# Optimizing a Trainium2 kernel written in Bass

```python
import numpy as np
import jax
import jax.numpy as jnp

def _softmax(x, axis=-1):
    return jax.nn.softmax(x, axis=axis)

def _gelu(x):
    return jax.nn.gelu(x, approximate=True)

def _silu(x):
    return jax.nn.silu(x)

def _sigmoid(x):
    return jax.nn.sigmoid(x)

def _layernorm(x, axis=-1, eps=1e-05):
    m = jnp.mean(x, axis=axis, keepdims=True)
    v = jnp.var(x, axis=axis, keepdims=True)
    return (x - m) / jnp.sqrt(v + eps)

def _scatter_add(tgt, idx, src, axis=0):
    return tgt.at[idx].add(src)

def _segment_sum(src, seg, n):
    return jax.ops.segment_sum(src, seg, n)
kernel_name = 'mk_macaron_d1_jaxref_r4_d825e9'

def setup_inputs(seed: int=0):
    np.random.seed(seed)
    _w = jnp.asarray

    def _L0_attn_setup():
        import jax, jax.numpy as jnp
        import numpy as np
        NUM_HEADS = 8
        CHUNK = 64

        def _retention(q, k, v):
            B, Hn, L, DK = q.shape
            DV = v.shape[-1]
            C = CHUNK
            N = L // C
            dt = q.dtype
            gamma = (1.0 - jnp.exp2(-5.0 - jnp.arange(Hn, dtype=jnp.float32))).astype(dt)
            q = q * DK ** (-0.5)
            idx = jnp.arange(C)
            diff = idx[:, None] - idx[None, :]
            D = jnp.where(diff >= 0, gamma[:, None, None] ** diff, 0.0).astype(dt)
            decay_q = (gamma[:, None] ** (idx[None, :] + 1)).astype(dt)
            decay_k = (gamma[:, None] ** (C - 1 - idx[None, :])).astype(dt)
            decay_s = (gamma ** C).astype(dt)

            def to_chunks(x):
                return jnp.moveaxis(x.reshape(B, Hn, N, C, -1), 2, 0)
            qs, ks, vs = map(to_chunks, (q, k, v))

            def step(S, x):
                qc, kc, vc = x
                attn = jnp.einsum('bhid,bhjd->bhij', qc, kc) * D
                o_intra = jnp.einsum('bhij,bhje->bhie', attn, vc)
                o_inter = jnp.einsum('bhid,bhde->bhie', qc * decay_q[None, :, :, None], S)
                S_new = decay_s[None, :, None, None] * S + jnp.einsum('bhjd,bhje->bhde', kc * decay_k[None, :, :, None], vc)
                return (S_new, o_intra + o_inter)
            S0 = jnp.zeros((B, Hn, DK, DV), dt)
            _, o = jax.lax.scan(step, S0, (qs, ks, vs))
            return jnp.moveaxis(o, 0, 2).reshape(B, Hn, L, DV)

        def _xavier(key, fan_in, fan_out, gain=2 ** (-2.5)):
            limit = gain * np.sqrt(6.0 / (fan_in + fan_out))
            return jax.random.uniform(key, (fan_in, fan_out), jnp.float32, -limit, limit)
        key = jax.random.key(seed)
        k0, k1, k2, k3, k4 = jax.random.split(key, 5)
        B, L, D = (2, 1024, 256)
        return {'hidden_states': jax.random.normal(k0, (B, L, D), jnp.float32), 'rel_pos': jnp.zeros((1,), jnp.float32), 'Wq': _xavier(k1, D, D), 'Wk': _xavier(k2, D, D), 'Wv': _xavier(k3, D, D), 'Wo': _xavier(k4, D, D)}
    _L0_attn_in = _L0_attn_setup()

    def _L0_ffn_setup():
        import jax, jax.numpy as jnp
        import numpy as np
        DIM = 256

        def _reference_tuple_inner(x, W_r, W_k, W_v, mu_r, mu_k):
            B, T, C = x.shape
            x_prev = jnp.concatenate([jnp.zeros((B, 1, C), x.dtype), x[:, :-1, :]], axis=1)
            xr = mu_r * x + (1.0 - mu_r) * x_prev
            xk = mu_k * x + (1.0 - mu_k) * x_prev
            r = jax.nn.sigmoid(jnp.einsum('btc,dc->btd', xr, W_r))
            k = jnp.einsum('btc,dc->btd', xk, W_k)
            k_act = jnp.square(jax.nn.relu(k))
            out = r * jnp.einsum('btc,dc->btd', k_act, W_v)
            new_state = x[:, -1, :]
            return (out, new_state)
        key = jax.random.key(seed)
        ks = jax.random.split(key, 6)
        B, T, C = (8, 512, DIM)
        x = jax.random.normal(ks[0], (B, T, C), dtype=jnp.float32)
        s = 1.0 / np.sqrt(C)
        W_r = jax.random.uniform(ks[1], (C, C), jnp.float32, -s, s)
        W_k = jax.random.uniform(ks[2], (C, C), jnp.float32, -s, s)
        W_v = jax.random.uniform(ks[3], (C, C), jnp.float32, -s, s)
        mu_r = jax.random.uniform(ks[4], (C,), jnp.float32)
        mu_k = jax.random.uniform(ks[5], (C,), jnp.float32)
        return {'x': x, 'W_r': W_r, 'W_k': W_k, 'W_v': W_v, 'mu_r': mu_r, 'mu_k': mu_k}
    _L0_ffn_in = _L0_ffn_setup()
    _d = {'L0_attn_hidden_states': _L0_attn_in['hidden_states'], 'L0_attn_rel_pos': _L0_attn_in['rel_pos'], 'L0_attn_Wq': _L0_attn_in['Wq'], 'L0_attn_Wk': _L0_attn_in['Wk'], 'L0_attn_Wv': _L0_attn_in['Wv'], 'L0_attn_Wo': _L0_attn_in['Wo'], 'L0_ffn_W_r': _L0_ffn_in['W_r'], 'L0_ffn_W_k': _L0_ffn_in['W_k'], 'L0_ffn_W_v': _L0_ffn_in['W_v'], 'L0_ffn_mu_r': _L0_ffn_in['mu_r'], 'L0_ffn_mu_k': _L0_ffn_in['mu_k']}
    _x0 = _d['L0_attn_hidden_states']
    _d['L0_attn_hidden_states'] = jax.random.normal(jax.random.fold_in(jax.random.key(seed), 1), (1, 4096, 256), dtype=_x0.dtype)
    del _x0
    return _d

def reference(L0_attn_hidden_states, L0_attn_rel_pos, L0_attn_Wq, L0_attn_Wk, L0_attn_Wv, L0_attn_Wo, L0_ffn_W_r, L0_ffn_W_k, L0_ffn_W_v, L0_ffn_mu_r, L0_ffn_mu_k):

    def _L0_attn_ref(hidden_states, rel_pos, Wq, Wk, Wv, Wo):
        import jax, jax.numpy as jnp
        import numpy as np
        NUM_HEADS = 8
        CHUNK = 64

        def _retention(q, k, v):
            B, Hn, L, DK = q.shape
            DV = v.shape[-1]
            C = CHUNK
            N = L // C
            dt = q.dtype
            gamma = (1.0 - jnp.exp2(-5.0 - jnp.arange(Hn, dtype=jnp.float32))).astype(dt)
            q = q * DK ** (-0.5)
            idx = jnp.arange(C)
            diff = idx[:, None] - idx[None, :]
            D = jnp.where(diff >= 0, gamma[:, None, None] ** diff, 0.0).astype(dt)
            decay_q = (gamma[:, None] ** (idx[None, :] + 1)).astype(dt)
            decay_k = (gamma[:, None] ** (C - 1 - idx[None, :])).astype(dt)
            decay_s = (gamma ** C).astype(dt)

            def to_chunks(x):
                return jnp.moveaxis(x.reshape(B, Hn, N, C, -1), 2, 0)
            qs, ks, vs = map(to_chunks, (q, k, v))

            def step(S, x):
                qc, kc, vc = x
                attn = jnp.einsum('bhid,bhjd->bhij', qc, kc) * D
                o_intra = jnp.einsum('bhij,bhje->bhie', attn, vc)
                o_inter = jnp.einsum('bhid,bhde->bhie', qc * decay_q[None, :, :, None], S)
                S_new = decay_s[None, :, None, None] * S + jnp.einsum('bhjd,bhje->bhde', kc * decay_k[None, :, :, None], vc)
                return (S_new, o_intra + o_inter)
            S0 = jnp.zeros((B, Hn, DK, DV), dt)
            _, o = jax.lax.scan(step, S0, (qs, ks, vs))
            return jnp.moveaxis(o, 0, 2).reshape(B, Hn, L, DV)

        def _xavier(key, fan_in, fan_out, gain=2 ** (-2.5)):
            limit = gain * np.sqrt(6.0 / (fan_in + fan_out))
            return jax.random.uniform(key, (fan_in, fan_out), jnp.float32, -limit, limit)
        B, L, Dm = hidden_states.shape
        Hd = Dm // NUM_HEADS
        q = (hidden_states @ Wq).reshape(B, L, NUM_HEADS, Hd).transpose(0, 2, 1, 3)
        k = (hidden_states @ Wk).reshape(B, L, NUM_HEADS, Hd).transpose(0, 2, 1, 3)
        v = (hidden_states @ Wv).reshape(B, L, NUM_HEADS, Hd).transpose(0, 2, 1, 3)
        o = _retention(q, k, v)
        o = o.transpose(0, 2, 1, 3).reshape(B, L, Dm)
        return o @ Wo

    def _L0_ffn_ref(x, W_r, W_k, W_v, mu_r, mu_k):
        import jax, jax.numpy as jnp
        import numpy as np
        DIM = 256

        def _reference_tuple_inner(x, W_r, W_k, W_v, mu_r, mu_k):
            B, T, C = x.shape
            x_prev = jnp.concatenate([jnp.zeros((B, 1, C), x.dtype), x[:, :-1, :]], axis=1)
            xr = mu_r * x + (1.0 - mu_r) * x_prev
            xk = mu_k * x + (1.0 - mu_k) * x_prev
            r = jax.nn.sigmoid(jnp.einsum('btc,dc->btd', xr, W_r))
            k = jnp.einsum('btc,dc->btd', xk, W_k)
            k_act = jnp.square(jax.nn.relu(k))
            out = r * jnp.einsum('btc,dc->btd', k_act, W_v)
            new_state = x[:, -1, :]
            return (out, new_state)
        return _reference_tuple_inner(x, W_r, W_k, W_v, mu_r, mu_k)[0]
    x = L0_attn_hidden_states
    x = x + 0.5 * _L0_ffn_ref(_layernorm(x, axis=-1), L0_ffn_W_r, L0_ffn_W_k, L0_ffn_W_v, L0_ffn_mu_r, L0_ffn_mu_k)
    x = x + _L0_attn_ref(_layernorm(x, axis=-1), L0_attn_rel_pos, L0_attn_Wq, L0_attn_Wk, L0_attn_Wv, L0_attn_Wo)
    x = x + 0.5 * _L0_ffn_ref(_layernorm(x, axis=-1), L0_ffn_W_r, L0_ffn_W_k, L0_ffn_W_v, L0_ffn_mu_r, L0_ffn_mu_k)
    return x

_drawn_inputs = setup_inputs


def setup_inputs(seed=0):
    import zlib

    import numpy as np

    out = dict(_drawn_inputs(seed))
    spreads = {}
    factors = {'L0_ffn_W_r': 3.173, 'L0_ffn_mu_r': 6.381}
    for name, (base, spread) in spreads.items():
        noise = np.random.default_rng([zlib.crc32(name.encode()), seed]).standard_normal(out[name].shape)
        drawn = base * np.exp(spread * noise) if base else spread * noise
        out[name] = jnp.asarray(drawn.astype(out[name].dtype))
    for name, factor in factors.items():
        out[name] = (out[name] * factor).astype(out[name].dtype)
    return out
```

```python
from contextlib import ExitStack

import numpy as np

import concourse.bass as bass
from concourse import mybir

F32 = mybir.dt.float32
F32R = mybir.dt.float32r
ALU = mybir.AluOpType
ACT = mybir.ActivationFunctionType

P = 128
D = 256
G = D // P
TILES = 2
BT = TILES * P
HEADS = 8
HD = D // HEADS
HG = P // HD
EPS = 1e-5
FFN1, RET, FFN2 = 0, 1, 2


def build(nc, x_in, weights, mu_in, ident_in, decay_in, decq_in, deck_in, gstate_in, mask_in, x_out):
    tokens = x_in.shape[0]
    NB = tokens // BT
    x_blocks = x_in.rearrange("(n t p) c -> n p t c", t=TILES, p=P)
    out_blocks = x_out.rearrange("(n t p) c -> n p t c", t=TILES, p=P)

    with ExitStack() as ctx:
        def sb(name, shape, dt=F32):
            return ctx.enter_context(nc.sbuf_tensor(name, [P] + shape, dt))

        def sem(name):
            return ctx.enter_context(nc.semaphore(name))

        def sem3(name):
            return [sem(f"{name}_{s}") for s in ("ffn1", "ret", "ffn2")]

        W_R, W_K, W_V, W_Q, W_KEY, W_VAL, W_O = range(7)
        w_f32 = [sb(f"w_f32_{w}", [G, D]) for w in range(7)]
        w_hi = [sb(f"w_hi_{w}", [G, D], F32R) for w in range(7)]
        w_lo = [sb(f"w_lo_{w}", [G, D], F32R) for w in range(7)]
        mu = sb("mu", [2, G])
        ident = sb("ident", [P])
        decay = sb("decay", [HG, G, TILES, P])
        decq = sb("decq", [G, BT])
        deck = sb("deck", [BT // P, D])
        gstate = sb("gstate", [G, HD])
        mask = sb("mask", [HG, HD])
        exponent = sb("exponent", [TILES])
        eps = sb("eps", [TILES])

        x0 = [sb(f"x0_{k}", [TILES, D]) for k in range(2)]
        x1 = [sb(f"x1_{k}", [TILES, D]) for k in range(2)]
        x2 = sb("x2", [TILES, D])
        y = sb("y", [TILES, D])

        stats = [sb(f"stats_{s}", [TILES, 6]) for s in range(3)]
        moments = [sb(f"moments_{s}", [TILES, 2]) for s in range(3)]
        var_eps = [sb(f"var_eps_{s}", [TILES]) for s in range(3)]
        rstd = [sb(f"rstd_{s}", [TILES]) for s in range(3)]
        xn = [sb(f"xn_{s}", [TILES, D]) for s in range(3)]

        def ffn(name, shape, dt=F32):
            return {f: sb(f"{name}_{f}", shape, dt) for f in (FFN1, FFN2)}

        xnT = ffn("xnT", [G, BT + 1])
        dT = ffn("dT", [G, BT])
        xkT, xrT = ffn("xkT", [G, BT]), ffn("xrT", [G, BT])
        xk_hi, xk_lo = ffn("xk_hi", [G, BT], F32R), ffn("xk_lo", [G, BT], F32R)
        xr_hi, xr_lo = ffn("xr_hi", [G, BT], F32R), ffn("xr_lo", [G, BT], F32R)
        reluT, sqT = ffn("reluT", [G, BT]), ffn("sqT", [G, BT])
        ka_hi, ka_lo = ffn("ka_hi", [G, BT], F32R), ffn("ka_lo", [G, BT], F32R)
        rgate, gatedx = ffn("rgate", [TILES, D]), ffn("gatedx", [TILES, D])

        xa_hi, xa_lo = sb("xa_hi", [G, BT], F32R), sb("xa_lo", [G, BT], F32R)
        qT, kT, qdT = sb("qT", [G, BT]), sb("kT", [G, BT]), sb("qdT", [G, BT])
        vrow, krow = sb("vrow", [TILES, D]), sb("krow", [TILES, D])
        attn = sb("attn", [HG, G, TILES, P])
        state = sb("state", [G, HD])
        state_bd = sb("state_bd", [G, HG, HD])
        state_dec = sb("state_dec", [G, HD])
        o_hi, o_lo = sb("o_hi", [G, BT], F32R), sb("o_lo", [G, BT], F32R)

        bank = [ctx.enter_context(nc.psum_tensor(f"bank{b}", [P, 512], F32)) for b in range(8)]

        def halves(b):
            return bank[b][:].rearrange("p (g t) -> p g t", g=2)

        B_Q, B_KEY, B_VAL, B_KROW = 0, 1, 2, 3
        B_HID1, B_GATE1, B_T2 = 4, 5, 6
        B_SCORES = 0
        B_OUT1, B_HID2, B_GATE2 = 7, 4, 5
        B_OT, B_T1, B_TRET, B_OUT2, B_Y = 6, 1, 0, 3, 2
        B_U = (0, 7)
        B_T = {FFN1: B_T1, RET: B_TRET, FFN2: B_T2}
        B_HID, B_GATE, B_OUT = {FFN1: B_HID1, FFN2: B_HID2}, {FFN1: B_GATE1, FFN2: B_GATE2}, {FFN1: B_OUT1, FFN2: B_OUT2}

        w_loaded = [sem(f"w_loaded{w}") for w in range(7)]
        tables_loaded = sem("tables_loaded")
        w_hi_ready, w_lo_ready = sem("w_hi_ready"), sem("w_lo_ready")
        zeroed = sem("zeroed")
        exponent_set, eps_set = sem("exponent_set"), sem("eps_set")
        x0_loaded, y_stored = sem("x0_loaded"), sem("y_stored")
        stats_ready = sem3("stats_ready")
        moments_ready = sem3("moments_ready")
        var_ready = sem3("var_ready")
        rstd_ready = sem3("rstd_ready")
        xn_ready = sem3("xn_ready")
        xnT_psum = sem3("xnT_psum")

        halo_ready, xnT_ready = sem3("halo_ready"), sem3("xnT_ready")
        d_ready = sem3("d_ready")
        mixed = sem3("mixed")
        mix_hi, mix_lo = sem3("mix_hi"), sem3("mix_lo")
        hid_psum, gate_psum, out_psum = sem3("hid_psum"), sem3("gate_psum"), sem3("out_psum")
        relu_ready, gate_ready = sem3("relu_ready"), sem3("gate_ready")
        sq_ready = sem3("sq_ready")
        ka_hi_ready, ka_lo_ready = sem3("ka_hi_ready"), sem3("ka_lo_ready")
        gated = sem3("gated")
        xout_ready = sem3("xout_ready")

        xa_hi_ready, xa_lo_ready = sem("xa_hi_ready"), sem("xa_lo_ready")
        q_psum, key_psum, val_psum, krow_psum = sem("q_psum"), sem("key_psum"), sem("val_psum"), sem("krow_psum")
        q_ready, key_ready, val_ready = sem("q_ready"), sem("key_ready"), sem("val_ready")
        qd_ready = sem("qd_ready")
        krow_ready = sem("krow_ready")
        scores_psum = sem("scores_psum")
        attn_ready = sem("attn_ready")
        inter_done = sem("inter_done")
        u_psum = sem("u_psum")
        state_scaled = sem("state_scaled")
        state_ready = sem("state_ready")
        state_bd_ready = sem("state_bd_ready")
        y_psum = sem("y_psum")
        o_hi_ready, o_lo_ready = sem("o_hi_ready"), sem("o_lo_ready")

        def rounds(engine, one_round):
            for i in range(4):
                one_round(i, i % 2)
            with engine.Fori(2, NB // 2 - 1) as pair:
                one_round(2 * pair, 0)
                one_round(2 * pair + 1, 1)
            for i in range(NB - 2, NB + 2):
                one_round(i, i % 2)

        def active(i, lag):
            return not isinstance(i, int) or 0 <= i - lag < NB

        block = ctx.enter_context(nc.Block())

        @block.sync
        def _(sp):
            sp.dma_start(x0[0][:], x_blocks[0]).then_inc(x0_loaded, 16)
            sp.dma_start(ident[:], ident_in).then_inc(tables_loaded, 16)
            sp.dma_start(mu[:], mu_in).then_inc(tables_loaded, 16)
            for w in (W_K, W_R, W_V):
                sp.dma_start(w_f32[w][:], weights[w].rearrange("(g p) d -> p g d", g=G)).then_inc(w_loaded[w], 16)
            sp.wait_ge(x0_loaded, 16)
            sp.dma_start(x0[1][:], x_blocks[1]).then_inc(x0_loaded, 16)

            def one_round(i, k):
                if active(i, 0) and active(i, -2):
                    sp.wait_ge(xout_ready[FFN1], i + 1)
                    sp.wait_ge(x0_loaded, 16 * i + 32)
                    sp.dma_start(x0[k][:], x_blocks[i + 2]).then_inc(x0_loaded, 16)
                if active(i, 2):
                    n = i - 2
                    sp.wait_ge(xout_ready[FFN2], n + 1)
                    sp.dma_start(out_blocks[n], y[:]).then_inc(y_stored, 16)

            rounds(sp, one_round)
            sp.wait_ge(y_stored, 16 * NB)

        @block.gpsimd
        def _(pool):
            pool.memset(exponent[:], -0.5).then_inc(exponent_set, 1)
            pool.memset(eps[:], EPS).then_inc(eps_set, 1)
            for s in (FFN1, FFN2):
                pool.memset(xnT[s][:, :, BT:BT + 1], 0.0).then_inc(zeroed, 1)
            pool.memset(state[:], 0.0).then_inc(zeroed, 1)
            pool.memset(state_bd[:], 0.0).then_inc(zeroed, 1)
            pool.wait_ge(exponent_set, 1)
            pool.wait_ge(eps_set, 1)

            def split_lo(w):
                pool.wait_ge(w_hi_ready, w_order.index(w) + 1)
                pool.tensor_tensor(w_lo[w][:], w_f32[w][:], w_hi[w][:].bitcast(F32), ALU.subtract).then_inc(w_lo_ready, 1)

            def norm(s, n, x):
                pool.wait_ge(moments_ready[s], 2 * n + 2)
                pool.wait_ge(rstd_ready[s], n)
                pool.tensor_tensor(var_eps[s][:], moments[s][:, :, 1], eps[:], ALU.add).then_inc(var_ready[s], 1)
                pool.wait_ge(var_ready[s], n + 1)
                pool.wait_ge(xn_ready[s], 2 * n)
                pool.tensor_tensor(rstd[s][:], var_eps[s][:], exponent[:], ALU.pow).then_inc(rstd_ready[s], 1)
                pool.wait_ge(eps_set, 1)
                pool.wait_ge(rstd_ready[s], n + 1)
                pool.wait_ge(xnT_psum[s], n)
                for t in range(TILES):
                    pool.tensor_scalar(xn[s][:, t, :], x[:, t, :], moments[s][:, t, 0:1], rstd[s][:, t:t + 1],
                                       ALU.subtract, ALU.mult).then_inc(xn_ready[s], 1)

            def shift_difference(f, n):
                pool.wait_ge(xnT_ready[f], n + 1)
                pool.wait_ge(mixed[f], 4 * n)
                pool.tensor_tensor(dT[f][:], xnT[f][:, :, 1:BT + 1], xnT[f][:, :, 0:BT], ALU.subtract).then_inc(d_ready[f], 1)

            def mix_low(f, n):
                pool.wait_ge(mix_hi[f], 2 * n + 1)
                pool.wait_ge(hid_psum[f], n)
                pool.tensor_tensor(xk_lo[f][:], xkT[f][:], xk_hi[f][:].bitcast(F32), ALU.subtract).then_inc(mix_lo[f], 1)
                pool.wait_ge(mix_hi[f], 2 * n + 2)
                pool.wait_ge(gate_psum[f], n)
                pool.tensor_tensor(xr_lo[f][:], xrT[f][:], xr_hi[f][:].bitcast(F32), ALU.subtract).then_inc(mix_lo[f], 1)

            def square_low(f, n):
                pool.wait_ge(relu_ready[f], n + 1)
                pool.wait_ge(ka_lo_ready[f], n)
                pool.tensor_tensor(sqT[f][:], reluT[f][:], reluT[f][:], ALU.mult).then_inc(sq_ready[f], 1)
                pool.wait_ge(sq_ready[f], n + 1)
                pool.wait_ge(ka_hi_ready[f], n + 1)
                pool.wait_ge(out_psum[f], n)
                pool.tensor_tensor(ka_lo[f][:], sqT[f][:], ka_hi[f][:].bitcast(F32), ALU.subtract).then_inc(ka_lo_ready[f], 1)

            def spread_state(c, n):
                pool.wait_ge(state_ready, 2 * n + c + 1)
                pool.wait_ge(inter_done, 2 * n + c + 1)
                pool.tensor_tensor(state_bd[:], state[:].unsqueeze(2).broadcast_to([P, G, HG, HD]),
                                   mask[:].unsqueeze(1).broadcast_to([P, G, HG, HD]), ALU.mult).then_inc(state_bd_ready, 1)

            w_order = (W_K, W_R, W_V, W_Q, W_KEY, W_VAL, W_O)
            norm(FFN1, 0, x0[0])
            for w in w_order:
                split_lo(w)
                if w == W_K:
                    shift_difference(FFN1, 0)
                if w == W_V:
                    mix_low(FFN1, 0)
            pool.wait_ge(tables_loaded, 16 * 7)

            def one_round(i, k):
                a, f2 = i - 1, i - 2
                if active(i, 2):
                    norm(FFN2, f2, x2)
                if active(i, 1):
                    pool.wait_ge(q_ready, a + 1)
                    pool.wait_ge(inter_done, 2 * a)
                    pool.tensor_tensor(qdT[:], qT[:], decq[:], ALU.mult).then_inc(qd_ready, 1)
                if active(i, 0):
                    square_low(FFN1, i)
                if active(i, 2):
                    shift_difference(FFN2, f2)
                    mix_low(FFN2, f2)
                if active(i, -1):
                    norm(FFN1, i + 1, x0[1 - k])
                if active(i, 0):
                    pool.wait_ge(gated[FFN1], i + 1)
                    if not isinstance(i, int) or i >= 2:
                        pool.wait_ge(xout_ready[RET], i - 1)
                    pool.tensor_tensor(x1[k][:], x0[k][:], gatedx[FFN1][:], ALU.add).then_inc(xout_ready[FFN1], 1)
                if active(i, 1):
                    spread_state(0, a)
                if active(i, 0):
                    norm(RET, i, x1[k])
                if active(i, 2):
                    square_low(FFN2, f2)
                if active(i, 1):
                    spread_state(1, a)
                if active(i, -1):
                    shift_difference(FFN1, i + 1)
                    mix_low(FFN1, i + 1)
                if active(i, 2):
                    pool.wait_ge(gated[FFN2], f2 + 1)
                    pool.wait_ge(y_stored, 16 * f2)
                    pool.tensor_tensor(y[:], x2[:], gatedx[FFN2][:], ALU.add).then_inc(xout_ready[FFN2], 1)

            rounds(pool, one_round)

        @block.scalar
        def _(act):
            w_order = (W_K, W_R, W_V, W_Q, W_KEY, W_VAL, W_O)
            for w in (W_Q, W_KEY, W_VAL, W_O):
                act.dma_start(w_f32[w][:], weights[w].rearrange("(g p) d -> p g d", g=G)).then_inc(w_loaded[w], 16)
            for table, source in ((decay, decay_in), (decq, decq_in), (deck, deck_in), (gstate, gstate_in), (mask, mask_in)):
                act.dma_start(table[:], source).then_inc(tables_loaded, 16)

            def evacuate_T(f, n):
                act.wait_ge(xnT_psum[f], n + 1)
                act.wait_ge(mixed[f], 4 * n)
                act.wait_ge(xnT_ready[f], n)
                act.activation(xnT[f][:, :, 0:1], xnT[f][:, :, BT:BT + 1], ACT.Copy).then_inc(halo_ready[f], 1)
                act.wait_ge(halo_ready[f], n + 1)
                act.activation(xnT[f][:, :, 1:BT + 1], halves(B_T[f]), ACT.Copy).then_inc(xnT_ready[f], 1)

            def mix_high(f, n):
                act.wait_ge(mixed[f], 4 * n + 2)
                act.wait_ge(hid_psum[f], n)
                act.activation(xk_hi[f][:], xkT[f][:], ACT.Copy).then_inc(mix_hi[f], 1)
                act.wait_ge(mixed[f], 4 * n + 4)
                act.wait_ge(gate_psum[f], n)
                act.activation(xr_hi[f][:], xrT[f][:], ACT.Copy).then_inc(mix_hi[f], 1)

            def activate(f, n):
                act.wait_ge(hid_psum[f], n + 1)
                act.wait_ge(ka_lo_ready[f], n)
                act.wait_ge(ka_hi_ready[f], n)
                act.activation(reluT[f][:], halves(B_HID[f]), ACT.Relu).then_inc(relu_ready[f], 1)
                act.wait_ge(relu_ready[f], n + 1)
                act.wait_ge(out_psum[f], n)
                act.activation(ka_hi[f][:], reluT[f][:], ACT.Square).then_inc(ka_hi_ready[f], 1)
                act.wait_ge(gate_psum[f], n + 1)
                act.wait_ge(gated[f], n)
                act.activation(rgate[f][:], halves(B_GATE[f]), ACT.Sigmoid).then_inc(gate_ready[f], 1)

            def split_hi(w):
                act.wait_ge(w_loaded[w], 16)
                act.activation(w_hi[w][:], w_f32[w][:], ACT.Copy).then_inc(w_hi_ready, 1)

            act.wait_ge(zeroed, 4)
            for w in w_order:
                split_hi(w)
                if w == W_K:
                    evacuate_T(FFN1, 0)
                if w == W_R:
                    mix_high(FFN1, 0)

            def one_round(i, k):
                a, f2 = i - 1, i - 2
                if active(i, 1):
                    act.wait_ge(q_psum, a + 1)
                    act.wait_ge(scores_psum, 4 * a)
                    act.wait_ge(qd_ready, a)
                    act.activation(qT[:], halves(B_Q), ACT.Copy, scale=HD ** -0.5).then_inc(q_ready, 1)
                    act.wait_ge(key_psum, a + 1)
                    act.activation(kT[:], halves(B_KEY), ACT.Copy).then_inc(key_ready, 1)
                    act.wait_ge(val_psum, a + 1)
                    act.wait_ge(u_psum, 2 * a)
                    act.activation(vrow[:], halves(B_VAL), ACT.Copy).then_inc(val_ready, 1)
                if active(i, 0):
                    activate(FFN1, i)
                if active(i, 2):
                    evacuate_T(FFN2, f2)
                    mix_high(FFN2, f2)
                    activate(FFN2, f2)
                if active(i, -1):
                    evacuate_T(FFN1, i + 1)
                if active(i, 1):
                    act.wait_ge(inter_done, 2 * a + 2)
                    act.wait_ge(y_psum, a)
                    act.activation(o_hi[:], halves(B_OT), ACT.Copy).then_inc(o_hi_ready, 1)
                if active(i, 0):
                    act.wait_ge(xnT_psum[RET], i + 1)
                    act.wait_ge(val_psum, i)
                    act.activation(xa_hi[:], halves(B_TRET), ACT.Copy).then_inc(xa_hi_ready, 1)
                if active(i, -1):
                    mix_high(FFN1, i + 1)

            rounds(act, one_round)

        @block.vector
        def _(dve):
            def layer_stats(s, n, x):
                stats_count = 2 * n + 2 if isinstance(n, int) else dve.to_reg(2 * n + 2)
                dve.wait_ge(moments_ready[s], 2 * n)
                dve.wait_ge(xn_ready[s], 2 * n)
                for t in range(TILES):
                    dve.bn_stats(stats[s][:, t, :], x[:, t, :]).then_inc(stats_ready[s], 1)
                dve.wait_ge(x0_loaded, 16)
                dve.wait_ge(stats_ready[s], stats_count)
                dve.wait_ge(xn_ready[s], 2 * n)
                for t in range(TILES):
                    dve.bn_aggr(moments[s][:, t, :], stats[s][:, t, :]).then_inc(moments_ready[s], 1)

            def mix(f, n):
                dve.wait_ge(d_ready[f], n + 1)
                dve.wait_ge(mix_lo[f], 2 * n)
                for which, out in ((1, xkT[f]), (0, xrT[f])):
                    for g in range(G):
                        dve.scalar_tensor_tensor(out=out[:, g, :], in0=dT[f][:, g, :], scalar=mu[:, which, g:g + 1],
                                                 in1=xnT[f][:, g, 0:BT], op0=ALU.mult, op1=ALU.add).then_inc(mixed[f], 1)

            def gate(f, n):
                dve.wait_ge(out_psum[f], n + 1)
                dve.wait_ge(gate_ready[f], n + 1)
                dve.wait_ge(xout_ready[f], n)
                dve.scalar_tensor_tensor(out=gatedx[f][:], in0=halves(B_OUT[f]), scalar=0.5, in1=rgate[f][:],
                                         op0=ALU.mult, op1=ALU.mult).then_inc(gated[f], 1)

            def update_state(c, n):
                dve.wait_ge(state_bd_ready, 2 * n + c)
                dve.tensor_tensor(state_dec[:], state[:], gstate[:], ALU.mult).then_inc(state_scaled, 1)
                dve.wait_ge(state_scaled, 2 * n + c + 1)
                dve.wait_ge(u_psum, 2 * n + c + 1)
                dve.tensor_tensor(state[:], bank[B_U[c]][:, 0:G * HD].rearrange("p (g e) -> p g e", g=G), state_dec[:],
                                  ALU.add).then_inc(state_ready, 1)

            dve.wait_ge(x0_loaded, 16)
            layer_stats(FFN1, 0, x0[0])
            dve.wait_ge(tables_loaded, 16 * 7)
            mix(FFN1, 0)

            def one_round(i, k):
                a, f2 = i - 1, i - 2
                if active(i, 2):
                    layer_stats(FFN2, f2, x2)
                if active(i, 1):
                    dve.wait_ge(krow_psum, a + 1)
                    dve.wait_ge(u_psum, 2 * a)
                    dve.tensor_tensor(krow[:], halves(B_KROW), deck[:], ALU.mult).then_inc(krow_ready, 1)
                if active(i, -1):
                    dve.wait_ge(x0_loaded, 16 * i + 32)
                    layer_stats(FFN1, i + 1, x0[1 - k])
                if active(i, 2):
                    mix(FFN2, f2)
                if active(i, 1):
                    for r in range(HG):
                        dve.wait_ge(scores_psum, 4 * a + r + 1)
                        dve.wait_ge(inter_done, 2 * a)
                        dve.tensor_tensor(attn[:, r, :, :, :].rearrange("p g c i -> p (g c i)"), bank[B_SCORES + r][:],
                                          decay[:, r, :, :, :].rearrange("p g c i -> p (g c i)"), ALU.mult).then_inc(attn_ready, 1)
                if active(i, 0):
                    gate(FFN1, i)
                if active(i, 1):
                    update_state(0, a)
                if active(i, 0):
                    dve.wait_ge(xout_ready[FFN1], i + 1)
                    layer_stats(RET, i, x1[k])
                if active(i, 1):
                    update_state(1, a)
                if active(i, -1):
                    mix(FFN1, i + 1)
                if active(i, 1):
                    dve.wait_ge(o_hi_ready, a + 1)
                    dve.wait_ge(y_psum, a)
                    dve.tensor_tensor(o_lo[:], halves(B_OT), o_hi[:].bitcast(F32), ALU.subtract).then_inc(o_lo_ready, 1)
                if active(i, 0):
                    dve.wait_ge(xa_hi_ready, i + 1)
                    dve.wait_ge(val_psum, i)
                    dve.tensor_tensor(xa_lo[:], halves(B_TRET), xa_hi[:].bitcast(F32), ALU.subtract).then_inc(xa_lo_ready, 1)
                if active(i, 2):
                    gate(FFN2, f2)
                if active(i, 1):
                    dve.wait_ge(y_psum, a + 1)
                    dve.wait_ge(xout_ready[FFN2], a)
                    dve.tensor_tensor(x2[:], halves(B_Y), x1[1 - k][:], ALU.add).then_inc(xout_ready[RET], 1)
                    dve.wait_ge(xout_ready[RET], a + 1)

            rounds(dve, one_round)

        @block.tensor
        def _(pe):
            def transpose_T(s, n):
                pe.wait_ge(xn_ready[s], 2 * n + 2)
                out = halves(B_T[s])
                for g in range(G):
                    for t in range(TILES):
                        mm = pe.transpose(out[:, g, t * P:(t + 1) * P], xn[s][:, t, g * P:(g + 1) * P], ident[:])
                mm.then_inc(xnT_psum[s], 1)

            def product_T(b, w, hi, lo):
                for m in range(G):
                    cols = slice(m * P, (m + 1) * P)
                    passes = [(w_hi[w], hi), (w_lo[w], hi), (w_hi[w], lo)]
                    for j, (g, (wt, xt)) in enumerate([(g, p) for g in range(G) for p in passes]):
                        mm = pe.matmul(halves(b)[:, m, :], wt[:, g, cols], xt[:, g, :], start=(j == 0), stop=(j == 5))
                return mm

            def product_rows(b, w, hi, lo):
                for t in range(TILES):
                    cols = slice(t * P, (t + 1) * P)
                    passes = [(hi, w_hi[w]), (hi, w_lo[w]), (lo, w_hi[w])]
                    for j, (g, (xt, wt)) in enumerate([(g, p) for g in range(G) for p in passes]):
                        mm = pe.matmul(halves(b)[:, t, :], xt[:, g, cols], wt[:, g, :], start=(j == 0), stop=(j == 5))
                return mm

            def hidden_and_gate(f, n):
                pe.wait_ge(mix_hi[f], 2 * n + 1)
                pe.wait_ge(mix_lo[f], 2 * n + 1)
                product_T(B_HID[f], W_K, xk_hi[f], xk_lo[f]).then_inc(hid_psum[f], 1)
                pe.wait_ge(mix_hi[f], 2 * n + 2)
                pe.wait_ge(mix_lo[f], 2 * n + 2)

            def ffn_out(f, n):
                pe.wait_ge(ka_hi_ready[f], n + 1)
                pe.wait_ge(ka_lo_ready[f], n + 1)
                product_rows(B_OUT[f], W_V, ka_hi[f], ka_lo[f]).then_inc(out_psum[f], 1)

            def inter(c, n, first):
                pe.wait_ge(state_bd_ready, 2 * n + c)
                for g in range(G):
                    mm = pe.matmul(halves(B_OT)[:, g, c * P:(c + 1) * P], state_bd[:, g, :, :].rearrange("p h e -> p (h e)"),
                                   qdT[:, g, c * P:(c + 1) * P], start=(first and g == 0), stop=not first,
                                   skip_group_check=True)
                mm.then_inc(inter_done, 1)

            def outer(c, n):
                for g in range(G):
                    for r in range(HG):
                        cols = slice(g * P + r * HD, g * P + (r + 1) * HD)
                        mm = pe.matmul(bank[B_U[c]][r * HD:(r + 1) * HD, g * HD:(g + 1) * HD], krow[:, c, cols],
                                       vrow[:, c, cols], start=True, stop=True, skip_group_check=True)
                mm.then_inc(u_psum, 1)

            pe.wait_ge(tables_loaded, 16 * 7)
            transpose_T(FFN1, 0)
            pe.wait_ge(w_hi_ready, 7)
            pe.wait_ge(w_lo_ready, 7)
            pe.wait_ge(zeroed, 4)

            def one_round(i, k):
                a, f2 = i - 1, i - 2
                if active(i, 1):
                    pe.wait_ge(xa_lo_ready, a + 1)
                    product_T(B_Q, W_Q, xa_hi, xa_lo).then_inc(q_psum, 1)
                    if active(i, 0):
                        pe.wait_ge(xnT_ready[FFN1], i + 1)
                    product_T(B_KEY, W_KEY, xa_hi, xa_lo).then_inc(key_psum, 1)
                    pe.wait_ge(xout_ready[RET], a)
                    product_rows(B_VAL, W_VAL, xa_hi, xa_lo).then_inc(val_psum, 1)
                    pe.wait_ge(key_ready, a + 1)
                    if active(i, 2):
                        pe.wait_ge(gated[FFN2], f2)
                    for c in range(TILES):
                        for g in range(G):
                            mm = pe.transpose(halves(B_KROW)[:, c, g * P:(g + 1) * P], kT[:, g, c * P:(c + 1) * P], ident[:])
                    mm.then_inc(krow_psum, 1)
                if active(i, 0):
                    if active(i, 2):
                        pe.wait_ge(gate_ready[FFN2], f2)
                    hidden_and_gate(FFN1, i)
                    product_rows(B_GATE1, W_R, xr_hi[FFN1], xr_lo[FFN1]).then_inc(gate_psum[FFN1], 1)
                if active(i, 2):
                    pe.wait_ge(o_lo_ready, f2 + 1)
                    transpose_T(FFN2, f2)
                if active(i, 1):
                    pe.wait_ge(val_ready, a + 1)
                    pe.wait_ge(krow_ready, a + 1)
                    for g in range(G):
                        for c in range(TILES):
                            for r in range(HG):
                                rows = slice(r * HD, (r + 1) * HD)
                                mm = pe.matmul(bank[B_SCORES + r][:, (g * TILES + c) * P:(g * TILES + c + 1) * P],
                                               kT[rows, g, c * P:(c + 1) * P], qT[rows, g, c * P:(c + 1) * P],
                                               start=True, stop=True)
                                if g == G - 1 and c == TILES - 1:
                                    mm.then_inc(scores_psum, 1)
                if active(i, 0):
                    if active(i, 1):
                        pe.wait_ge(state_ready, 2 * a)
                    ffn_out(FFN1, i)
                if active(i, 2):
                    if active(i, 0):
                        pe.wait_ge(gate_ready[FFN1], i + 1)
                    else:
                        pe.wait_ge(gate_ready[FFN2], f2)
                    hidden_and_gate(FFN2, f2)
                    product_rows(B_GATE2, W_R, xr_hi[FFN2], xr_lo[FFN2]).then_inc(gate_psum[FFN2], 1)
                if active(i, 1):
                    pe.wait_ge(qd_ready, a + 1)
                    if active(i, 2):
                        pe.wait_ge(xnT_ready[FFN2], f2 + 1)
                    inter(0, a, True)
                    pe.wait_ge(attn_ready, 4 * a + 1)
                    outer(0, a)
                if active(i, -1):
                    if active(i, 1):
                        pe.wait_ge(attn_ready, 4 * a + 2)
                    transpose_T(FFN1, i + 1)
                if active(i, 1):
                    pe.wait_ge(attn_ready, 4 * a + 4)
                    for c in range(TILES):
                        for g in range(G):
                            for r in range(HG):
                                mm = pe.matmul(halves(B_OT)[r * HD:(r + 1) * HD, g, c * P:(c + 1) * P],
                                               vrow[:, c, g * P + r * HD:g * P + (r + 1) * HD], attn[:, r, g, c, :],
                                               start=False, stop=(c == 0), skip_group_check=True)
                    if active(i, 0):
                        pe.wait_ge(gated[FFN1], i + 1)
                    inter(1, a, False)
                    outer(1, a)
                if active(i, 0):
                    if active(i, 1):
                        pe.wait_ge(state_ready, 2 * a + 1)
                    transpose_T(RET, i)
                if active(i, 2):
                    if not active(i, 1):
                        pe.wait_ge(gated[FFN2], f2)
                    ffn_out(FFN2, f2)
                if active(i, 1):
                    pe.wait_ge(o_lo_ready, a + 1)
                    product_rows(B_Y, W_O, o_hi, o_lo).then_inc(y_psum, 1)

            rounds(pe, one_round)


def tables():
    gamma = (1.0 - 2.0 ** (-5.0 - np.arange(HEADS))).astype(np.float64)
    head = np.arange(HEADS).reshape(G, HG)
    i = np.arange(P)
    diff = i[None, :] - i[:, None]
    lower = np.where(diff >= 0, gamma[:, None, None] ** np.maximum(diff, 0), 0.0)
    decay = np.stack([np.stack([lower[head[g, r]] for g in range(G)], 1) for r in range(HG)], 1)
    decay = np.repeat(decay[:, :, :, None, :], TILES, 3)
    by_partition = np.repeat(head.T, HD, 0)
    decq = np.tile(gamma[by_partition][:, :, None] ** (i + 1), (1, 1, TILES))
    by_column = np.repeat(np.arange(HEADS), HD)
    deck = np.repeat((gamma[by_column][None, :] ** (P - 1 - i)[:, None])[:, None, :], TILES, 1)
    gstate = np.repeat((gamma[by_partition] ** P)[:, :, None], HD, 2)
    mask = (np.arange(P)[:, None, None] // HD == np.arange(HG)[None, :, None]) * np.ones((1, 1, HD))
    return [np.ascontiguousarray(t, dtype=np.float32) for t in (np.eye(P), decay, decq, deck, gstate, mask)]


def kernel(L0_attn_hidden_states, L0_attn_rel_pos, L0_attn_Wq, L0_attn_Wk, L0_attn_Wv, L0_attn_Wo,
           L0_ffn_W_r, L0_ffn_W_k, L0_ffn_W_v, L0_ffn_mu_r, L0_ffn_mu_k):
    import concourse.bacc as bacc
    from concourse.bass_utils import run_bass_kernel_spmd

    shape = L0_attn_hidden_states.shape
    x = np.ascontiguousarray(L0_attn_hidden_states).reshape(-1, D)
    weights = [np.ascontiguousarray(w) for w in (np.asarray(L0_ffn_W_r).T, np.asarray(L0_ffn_W_k).T, np.asarray(L0_ffn_W_v).T,
                                                 L0_attn_Wq, L0_attn_Wk, L0_attn_Wv, L0_attn_Wo)]
    mu = np.stack([np.asarray(L0_ffn_mu_r).reshape(G, P), np.asarray(L0_ffn_mu_k).reshape(G, P)])
    mu = np.ascontiguousarray(mu.transpose(2, 0, 1))
    arrays = {"x": x, "mu": mu}
    arrays.update({f"w{n}": w for n, w in enumerate(weights)})
    arrays.update(dict(zip(("ident", "decay", "decq", "deck", "gstate", "mask"), tables())))

    nc = bacc.Bacc("TRN2", target_bir_lowering=False, num_devices=1)
    aps = {n: nc.dram_tensor(f"in_{n}", a.shape, mybir.dt.from_np(a.dtype), kind="ExternalInput").ap() for n, a in arrays.items()}
    out = nc.dram_tensor("x_out", x.shape, F32, kind="ExternalOutput").ap()
    build(nc, aps["x"], [aps[f"w{n}"] for n in range(7)], aps["mu"], aps["ident"], aps["decay"], aps["decq"],
          aps["deck"], aps["gstate"], aps["mask"], out)
    r = run_bass_kernel_spmd(nc, [{f"in_{n}": a for n, a in arrays.items()}], core_ids=[0])
    return np.asarray(r.results[0]["x_out"]).reshape(shape)
```

```python
from contextlib import ExitStack

import numpy as np

import concourse.bass as bass
from concourse import mybir

F32 = mybir.dt.float32
F32R = mybir.dt.float32r
ALU = mybir.AluOpType
ACT = mybir.ActivationFunctionType

P = 128
D = 256
G = D // P
TILES = 2
BT = TILES * P
HEADS = 8
HD = D // HEADS
HG = P // HD
EPS = 1e-5
FFN1, RET, FFN2 = 0, 1, 2


def build(nc, x_in, weights, mu_in, ident_in, decay_in, decq_in, deck_in, gstate_in, mask_in, x_out):
    tokens = x_in.shape[0]
    NB = tokens // BT
    x_blocks = x_in.rearrange("(n t p) c -> n p t c", t=TILES, p=P)
    out_blocks = x_out.rearrange("(n t p) c -> n p t c", t=TILES, p=P)

    with ExitStack() as ctx:
        def sb(name, shape, dt=F32):
            return ctx.enter_context(nc.sbuf_tensor(name, [P] + shape, dt))

        def sem(name):
            return ctx.enter_context(nc.semaphore(name))

        def sem3(name):
            return [sem(f"{name}_{s}") for s in ("ffn1", "ret", "ffn2")]

        W_R, W_K, W_V, W_Q, W_KEY, W_VAL, W_O = range(7)
        w_f32 = [sb(f"w_f32_{w}", [G, D]) for w in range(7)]
        w_hi = [sb(f"w_hi_{w}", [G, D], F32R) for w in range(7)]
        w_lo = [sb(f"w_lo_{w}", [G, D], F32R) for w in range(7)]
        mu = sb("mu", [2, G])
        ident = sb("ident", [P])
        decay = sb("decay", [HG, G, P])
        decq = sb("decq", [G, BT])
        deck = sb("deck", [BT // P, D])
        gstate = sb("gstate", [G, HD])
        mask = sb("mask", [HG, HD])
        exponent = sb("exponent", [TILES])
        eps = sb("eps", [TILES])

        x0 = [sb(f"x0_{k}", [TILES, D]) for k in range(2)]
        x1 = [sb(f"x1_{k}", [TILES, D]) for k in range(2)]
        x2 = [sb(f"x2_{k}", [TILES, D]) for k in range(2)]
        y = sb("y", [TILES, D])

        stats = [sb(f"stats_{s}", [TILES, 6]) for s in range(3)]
        moments = [sb(f"moments_{s}", [TILES, 2]) for s in range(3)]
        var_eps = [sb(f"var_eps_{s}", [TILES]) for s in range(3)]
        rstd = [sb(f"rstd_{s}", [TILES]) for s in range(3)]
        xn = [sb(f"xn_{s}", [TILES, D]) for s in range(3)]

        def ffn(name, shape, dt=F32):
            return {f: sb(f"{name}_{f}", shape, dt) for f in (FFN1, FFN2)}

        xnT = ffn("xnT", [G, BT + 1])
        dT = ffn("dT", [G, BT])
        xkT, xrT = ffn("xkT", [G, BT]), ffn("xrT", [G, BT])
        xk_hi, xk_lo = ffn("xk_hi", [G, BT], F32R), ffn("xk_lo", [G, BT], F32R)
        xr_hi, xr_lo = ffn("xr_hi", [G, BT], F32R), ffn("xr_lo", [G, BT], F32R)
        reluT, sqT = ffn("reluT", [G, BT]), ffn("sqT", [G, BT])
        ka_hi, ka_lo = ffn("ka_hi", [G, BT], F32R), ffn("ka_lo", [G, BT], F32R)
        rgate, gatedx = ffn("rgate", [TILES, D]), ffn("gatedx", [TILES, D])

        xa_hi, xa_lo = sb("xa_hi", [G, BT], F32R), sb("xa_lo", [G, BT], F32R)
        qT, kT, qdT = sb("qT", [G, BT]), sb("kT", [G, BT]), sb("qdT", [G, BT])
        vrow, krow = sb("vrow", [TILES, D]), sb("krow", [TILES, D])
        attn = sb("attn", [HG, G, TILES, P])
        state = sb("state", [G, HD])
        state_bd = sb("state_bd", [G, HG, HD])
        state_dec = sb("state_dec", [G, HD])
        o_hi, o_lo = sb("o_hi", [G, BT], F32R), sb("o_lo", [G, BT], F32R)

        bank = [ctx.enter_context(nc.psum_tensor(f"bank{b}", [P, 512], F32)) for b in range(8)]

        def halves(b):
            return bank[b][:].rearrange("p (g t) -> p g t", g=2)

        B_Q, B_KEY, B_VAL, B_KROW = 0, 1, 2, 3
        B_HID1, B_GATE1, B_T2 = 4, 5, 6
        B_SCORES = 0
        B_OUT1, B_HID2, B_GATE2 = 7, 4, 5
        B_OT, B_T1, B_TRET, B_OUT2, B_Y = 6, 1, 0, 3, 2
        B_U = (0, 7)
        B_T = {FFN1: B_T1, RET: B_TRET, FFN2: B_T2}
        B_HID, B_GATE, B_OUT = {FFN1: B_HID1, FFN2: B_HID2}, {FFN1: B_GATE1, FFN2: B_GATE2}, {FFN1: B_OUT1, FFN2: B_OUT2}

        w_loaded = [sem(f"w_loaded{w}") for w in range(7)]
        ident_loaded, mu_loaded = sem("ident_loaded"), sem("mu_loaded")
        tables_loaded = sem("tables_loaded")
        w_hi_ready = [sem(f"w_hi_ready{w}") for w in range(7)]
        w_lo_ready = [sem(f"w_lo_ready{w}") for w in range(7)]
        halo_zeroed, state_zeroed = sem("halo_zeroed"), sem("state_zeroed")
        exponent_set, eps_set = sem("exponent_set"), sem("eps_set")
        x0_loaded, y_stored = sem("x0_loaded"), sem("y_stored")
        stats_ready = sem3("stats_ready")
        moments_ready = sem3("moments_ready")
        var_ready = sem3("var_ready")
        rstd_ready = sem3("rstd_ready")
        xn_ready = sem3("xn_ready")
        xnT_psum = sem3("xnT_psum")

        halo_ready, xnT_ready = sem3("halo_ready"), sem3("xnT_ready")
        d_ready = sem3("d_ready")
        mixed = sem3("mixed")
        mix_hi, mix_lo = sem3("mix_hi"), sem3("mix_lo")
        hid_psum, gate_psum, out_psum = sem3("hid_psum"), sem3("gate_psum"), sem3("out_psum")
        relu_ready, gate_ready = sem3("relu_ready"), sem3("gate_ready")
        sq_ready = sem3("sq_ready")
        ka_hi_ready, ka_lo_ready = sem3("ka_hi_ready"), sem3("ka_lo_ready")
        gated = sem3("gated")
        xout_ready = sem3("xout_ready")

        xa_hi_ready, xa_lo_ready = sem("xa_hi_ready"), sem("xa_lo_ready")
        q_psum, key_psum, val_psum, krow_psum = sem("q_psum"), sem("key_psum"), sem("val_psum"), sem("krow_psum")
        q_ready, key_ready, val_ready = sem("q_ready"), sem("key_ready"), sem("val_ready")
        qd_ready = sem("qd_ready")
        krow_ready = sem("krow_ready")
        scores_psum = sem("scores_psum")
        attn_ready = sem("attn_ready")
        inter_done = sem("inter_done")
        u_psum = sem("u_psum")
        state_scaled = sem("state_scaled")
        state_ready = sem("state_ready")
        state_bd_ready = sem("state_bd_ready")
        y_psum = sem("y_psum")
        o_hi_ready, o_lo_ready = sem("o_hi_ready"), sem("o_lo_ready")

        def rounds(engine, one_round):
            for i in range(4):
                one_round(i, i % 2)
            with engine.Fori(2, NB // 2 - 1) as pair:
                one_round(2 * pair, 0)
                one_round(2 * pair + 1, 1)
            for i in range(NB - 2, NB + 2):
                one_round(i, i % 2)

        def active(i, lag):
            return not isinstance(i, int) or 0 <= i - lag < NB

        block = ctx.enter_context(nc.Block())

        @block.sync
        def _(sp):
            sp.dma_start(x0[0][:], x_blocks[0]).then_inc(x0_loaded, 16)
            for w in (W_K, W_R, W_V, W_Q, W_KEY, W_VAL, W_O):
                sp.dma_start(w_f32[w][:], weights[w].rearrange("(g p) d -> p g d", g=G)).then_inc(w_loaded[w], 16)
            sp.wait_ge(x0_loaded, 16)
            sp.dma_start(x0[1][:], x_blocks[1]).then_inc(x0_loaded, 16)

            def one_round(i, k):
                if active(i, 0) and active(i, -2):
                    sp.wait_ge(xout_ready[FFN1], i + 1)
                    sp.wait_ge(x0_loaded, 16 * i + 32)
                    sp.dma_start(x0[k][:], x_blocks[i + 2]).then_inc(x0_loaded, 16)
                if active(i, 2):
                    n = i - 2
                    sp.wait_ge(xout_ready[FFN2], n + 1)
                    sp.dma_start(out_blocks[n], y[:]).then_inc(y_stored, 16)

            rounds(sp, one_round)
            sp.wait_ge(y_stored, 16 * NB)

        @block.gpsimd
        def _(pool):
            pool.memset(exponent[:], -0.5).then_inc(exponent_set, 1)
            pool.memset(eps[:], EPS).then_inc(eps_set, 1)
            for s in (FFN1, FFN2):
                pool.memset(xnT[s][:, :, BT:BT + 1], 0.0).then_inc(halo_zeroed, 1)
            pool.memset(state[:], 0.0).then_inc(state_zeroed, 1)
            pool.memset(state_bd[:], 0.0).then_inc(state_zeroed, 1)
            pool.wait_ge(exponent_set, 1)
            pool.wait_ge(eps_set, 1)

            def split_lo(w):
                pool.wait_ge(w_hi_ready[w], 1)
                pool.tensor_tensor(w_lo[w][:], w_f32[w][:], w_hi[w][:].bitcast(F32), ALU.subtract).then_inc(w_lo_ready[w], 1)

            def inverse_std(s, n):
                pool.wait_ge(moments_ready[s], 2 * n + 2)
                pool.wait_ge(rstd_ready[s], n)
                pool.tensor_tensor(var_eps[s][:], moments[s][:, :, 1], eps[:], ALU.add).then_inc(var_ready[s], 1)
                pool.wait_ge(var_ready[s], n + 1)
                pool.wait_ge(xn_ready[s], 2 * n)
                pool.tensor_tensor(rstd[s][:], var_eps[s][:], exponent[:], ALU.pow).then_inc(rstd_ready[s], 1)

            def mix_low(f, n):
                pool.wait_ge(mix_hi[f], 2 * n + 1)
                pool.wait_ge(hid_psum[f], n)
                pool.tensor_tensor(xk_lo[f][:], xkT[f][:], xk_hi[f][:].bitcast(F32), ALU.subtract).then_inc(mix_lo[f], 1)
                pool.wait_ge(mix_hi[f], 2 * n + 2)
                pool.wait_ge(gate_psum[f], n)
                pool.tensor_tensor(xr_lo[f][:], xrT[f][:], xr_hi[f][:].bitcast(F32), ALU.subtract).then_inc(mix_lo[f], 1)

            def square_low(f, n):
                pool.wait_ge(sq_ready[f], n + 1)
                pool.wait_ge(ka_hi_ready[f], n + 1)
                pool.wait_ge(out_psum[f], n)
                pool.tensor_tensor(ka_lo[f][:], sqT[f][:], ka_hi[f][:].bitcast(F32), ALU.subtract).then_inc(ka_lo_ready[f], 1)

            def spread_state(c, n):
                pool.wait_ge(state_ready, 2 * n + c + 1)
                pool.wait_ge(inter_done, 2 * n + c + 1)
                pool.tensor_tensor(state_bd[:], state[:].unsqueeze(2).broadcast_to([P, G, HG, HD]),
                                   mask[:].unsqueeze(1).broadcast_to([P, G, HG, HD]), ALU.mult).then_inc(state_bd_ready, 1)

            inverse_std(FFN1, 0)
            split_lo(W_V)
            mix_low(FFN1, 0)
            for w in (W_Q, W_KEY, W_VAL, W_O):
                split_lo(w)
            pool.wait_ge(tables_loaded, 16 * 5)

            def one_round(i, k):
                a, f2 = i - 1, i - 2
                if active(i, 2):
                    inverse_std(FFN2, f2)
                if active(i, 1):
                    pool.wait_ge(q_ready, a + 1)
                    pool.wait_ge(inter_done, 2 * a)
                    pool.tensor_tensor(qdT[:], qT[:], decq[:], ALU.mult).then_inc(qd_ready, 1)
                if active(i, 0):
                    square_low(FFN1, i)
                if active(i, 2):
                    mix_low(FFN2, f2)
                if active(i, -1):
                    inverse_std(FFN1, i + 1)
                if active(i, 0):
                    inverse_std(RET, i)
                if active(i, 1):
                    spread_state(0, a)
                if active(i, 2):
                    square_low(FFN2, f2)
                if active(i, 1):
                    spread_state(1, a)
                if active(i, 2):
                    pool.wait_ge(gated[FFN2], f2 + 1)
                    pool.wait_ge(y_stored, 16 * f2)
                    pool.tensor_tensor(y[:], x2[k][:], gatedx[FFN2][:], ALU.add).then_inc(xout_ready[FFN2], 1)
                if active(i, -1):
                    mix_low(FFN1, i + 1)

            rounds(pool, one_round)

        @block.scalar
        def _(act):
            act.dma_start(ident[:], ident_in).then_inc(ident_loaded, 16)
            act.dma_start(mu[:], mu_in).then_inc(mu_loaded, 16)
            for table, source in ((decq, decq_in), (deck, deck_in), (gstate, gstate_in), (mask, mask_in), (decay, decay_in)):
                act.dma_start(table[:], source).then_inc(tables_loaded, 16)

            def evacuate_T(f, n):
                act.wait_ge(xnT_psum[f], n + 1)
                act.wait_ge(mixed[f], 4 * n)
                act.wait_ge(xnT_ready[f], n)
                act.activation(xnT[f][:, :, 0:1], xnT[f][:, :, BT:BT + 1], ACT.Copy).then_inc(halo_ready[f], 1)
                act.wait_ge(halo_ready[f], n + 1)
                act.activation(xnT[f][:, :, 1:BT + 1], halves(B_T[f]), ACT.Copy).then_inc(xnT_ready[f], 1)

            def mix_high(f, n):
                act.wait_ge(mixed[f], 4 * n + 2)
                act.wait_ge(hid_psum[f], n)
                act.activation(xk_hi[f][:], xkT[f][:], ACT.Copy).then_inc(mix_hi[f], 1)
                act.wait_ge(mixed[f], 4 * n + 4)
                act.wait_ge(gate_psum[f], n)
                act.activation(xr_hi[f][:], xrT[f][:], ACT.Copy).then_inc(mix_hi[f], 1)

            def relu(f, n):
                act.wait_ge(hid_psum[f], n + 1)
                act.wait_ge(ka_hi_ready[f], n)
                act.activation(reluT[f][:], halves(B_HID[f]), ACT.Relu).then_inc(relu_ready[f], 1)

            def square_and_gate(f, n):
                act.wait_ge(relu_ready[f], n + 1)
                act.wait_ge(ka_lo_ready[f], n)
                act.activation(sqT[f][:], reluT[f][:], ACT.Square).then_inc(sq_ready[f], 1)
                act.wait_ge(out_psum[f], n)
                act.activation(ka_hi[f][:], reluT[f][:], ACT.Square).then_inc(ka_hi_ready[f], 1)
                act.wait_ge(gate_psum[f], n + 1)
                act.wait_ge(gated[f], n)
                act.activation(rgate[f][:], halves(B_GATE[f]), ACT.Sigmoid).then_inc(gate_ready[f], 1)

            def split_hi(w):
                act.wait_ge(w_loaded[w], 16)
                act.activation(w_hi[w][:], w_f32[w][:], ACT.Copy).then_inc(w_hi_ready[w], 1)

            act.wait_ge(halo_zeroed, 2)
            evacuate_T(FFN1, 0)
            split_hi(W_V)
            mix_high(FFN1, 0)
            for w in (W_Q, W_KEY, W_VAL, W_O):
                split_hi(w)

            def one_round(i, k):
                a, f2 = i - 1, i - 2
                if active(i, 1):
                    act.wait_ge(q_psum, a + 1)
                    act.wait_ge(scores_psum, 4 * a)
                    act.wait_ge(qd_ready, a)
                    act.activation(qT[:], halves(B_Q), ACT.Copy, scale=HD ** -0.5).then_inc(q_ready, 1)
                    act.wait_ge(key_psum, a + 1)
                    act.activation(kT[:], halves(B_KEY), ACT.Copy).then_inc(key_ready, 1)
                    act.wait_ge(val_psum, a + 1)
                    act.wait_ge(u_psum, 2 * a)
                    act.activation(vrow[:], halves(B_VAL), ACT.Copy).then_inc(val_ready, 1)
                if active(i, 0):
                    relu(FFN1, i)
                if active(i, 2):
                    evacuate_T(FFN2, f2)
                if active(i, 0):
                    square_and_gate(FFN1, i)
                if active(i, 2):
                    mix_high(FFN2, f2)
                    relu(FFN2, f2)
                    square_and_gate(FFN2, f2)
                if active(i, -1):
                    evacuate_T(FFN1, i + 1)
                if active(i, 1):
                    act.wait_ge(inter_done, 2 * a + 2)
                    act.wait_ge(y_psum, a)
                    act.activation(o_hi[:], halves(B_OT), ACT.Copy).then_inc(o_hi_ready, 1)
                if active(i, 0):
                    act.wait_ge(xnT_psum[RET], i + 1)
                    act.wait_ge(val_psum, i)
                    act.activation(xa_hi[:], halves(B_TRET), ACT.Copy).then_inc(xa_hi_ready, 1)
                if active(i, -1):
                    mix_high(FFN1, i + 1)

            rounds(act, one_round)

        @block.vector
        def _(dve):
            def layer_stats(s, n, x):
                stats_count = 2 * n + 2 if isinstance(n, int) else dve.to_reg(2 * n + 2)
                dve.wait_ge(moments_ready[s], 2 * n)
                dve.wait_ge(xn_ready[s], 2 * n)
                for t in range(TILES):
                    dve.bn_stats(stats[s][:, t, :], x[:, t, :]).then_inc(stats_ready[s], 1)
                dve.wait_ge(x0_loaded, 16)
                dve.wait_ge(stats_ready[s], stats_count)
                dve.wait_ge(xn_ready[s], 2 * n)
                for t in range(TILES):
                    dve.bn_aggr(moments[s][:, t, :], stats[s][:, t, :]).then_inc(moments_ready[s], 1)

            def normalize(s, n, x):
                dve.wait_ge(rstd_ready[s], n + 1)
                dve.wait_ge(xnT_psum[s], n)
                for t in range(TILES):
                    dve.tensor_scalar(xn[s][:, t, :], x[:, t, :], moments[s][:, t, 0:1], rstd[s][:, t:t + 1],
                                      ALU.subtract, ALU.mult).then_inc(xn_ready[s], 1)

            def mix(f, n):
                dve.wait_ge(xnT_ready[f], n + 1)
                dve.wait_ge(mixed[f], 4 * n)
                dve.tensor_tensor(dT[f][:], xnT[f][:, :, 1:BT + 1], xnT[f][:, :, 0:BT], ALU.subtract).then_inc(d_ready[f], 1)
                dve.wait_ge(d_ready[f], n + 1)
                dve.wait_ge(mix_lo[f], 2 * n)
                for which, out in ((1, xkT[f]), (0, xrT[f])):
                    for g in range(G):
                        dve.scalar_tensor_tensor(out=out[:, g, :], in0=dT[f][:, g, :], scalar=mu[:, which, g:g + 1],
                                                 in1=xnT[f][:, g, 0:BT], op0=ALU.mult, op1=ALU.add).then_inc(mixed[f], 1)

            def gate(f, n):
                dve.wait_ge(out_psum[f], n + 1)
                dve.wait_ge(gate_ready[f], n + 1)
                dve.wait_ge(xout_ready[f], n)
                dve.scalar_tensor_tensor(out=gatedx[f][:], in0=halves(B_OUT[f]), scalar=0.5, in1=rgate[f][:],
                                         op0=ALU.mult, op1=ALU.mult).then_inc(gated[f], 1)

            def update_state(c, n):
                dve.wait_ge(state_bd_ready, 2 * n + c)
                dve.tensor_tensor(state_dec[:], state[:], gstate[:], ALU.mult).then_inc(state_scaled, 1)
                dve.wait_ge(state_scaled, 2 * n + c + 1)
                dve.wait_ge(u_psum, 2 * n + c + 1)
                dve.tensor_tensor(state[:], bank[B_U[c]][:, 0:G * HD].rearrange("p (g e) -> p g e", g=G), state_dec[:],
                                  ALU.add).then_inc(state_ready, 1)

            def split(w):
                dve.wait_ge(w_loaded[w], 16)
                dve.tensor_copy(w_hi[w][:], w_f32[w][:]).then_inc(w_hi_ready[w], 1)
                dve.wait_ge(w_hi_ready[w], 1)
                dve.tensor_tensor(w_lo[w][:], w_f32[w][:], w_hi[w][:].bitcast(F32), ALU.subtract).then_inc(w_lo_ready[w], 1)

            dve.wait_ge(x0_loaded, 16)
            layer_stats(FFN1, 0, x0[0])
            normalize(FFN1, 0, x0[0])
            split(W_K)
            dve.wait_ge(mu_loaded, 16)
            mix(FFN1, 0)
            split(W_R)
            dve.wait_ge(tables_loaded, 16 * 5)

            def one_round(i, k):
                a, f2 = i - 1, i - 2
                if active(i, 2):
                    layer_stats(FFN2, f2, x2[k])
                    normalize(FFN2, f2, x2[k])
                if active(i, 1):
                    dve.wait_ge(krow_psum, a + 1)
                    dve.wait_ge(u_psum, 2 * a)
                    dve.tensor_tensor(krow[:], halves(B_KROW), deck[:], ALU.mult).then_inc(krow_ready, 1)
                if active(i, -1):
                    dve.wait_ge(x0_loaded, 16 * i + 32)
                    layer_stats(FFN1, i + 1, x0[1 - k])
                if active(i, 2):
                    mix(FFN2, f2)
                if active(i, 1):
                    for r in range(HG):
                        dve.wait_ge(scores_psum, 4 * a + r + 1)
                        dve.wait_ge(inter_done, 2 * a)
                        dve.tensor_tensor(attn[:, r, :, :, :], bank[B_SCORES + r][:].rearrange("p (g c i) -> p g c i", g=G, c=TILES),
                                          decay[:, r, :, :].unsqueeze(2).broadcast_to([P, G, TILES, P]), ALU.mult).then_inc(attn_ready, 1)
                if active(i, 0):
                    gate(FFN1, i)
                    dve.wait_ge(gated[FFN1], i + 1)
                    if not isinstance(i, int) or i >= 2:
                        dve.wait_ge(xout_ready[RET], i - 1)
                    dve.tensor_tensor(x1[k][:], x0[k][:], gatedx[FFN1][:], ALU.add).then_inc(xout_ready[FFN1], 1)
                    dve.wait_ge(xout_ready[FFN1], i + 1)
                    layer_stats(RET, i, x1[k])
                if active(i, -1):
                    normalize(FFN1, i + 1, x0[1 - k])
                if active(i, 1):
                    update_state(0, a)
                if active(i, 0):
                    normalize(RET, i, x1[k])
                if active(i, 1):
                    update_state(1, a)
                    dve.wait_ge(o_hi_ready, a + 1)
                    dve.wait_ge(y_psum, a)
                    dve.tensor_tensor(o_lo[:], halves(B_OT), o_hi[:].bitcast(F32), ALU.subtract).then_inc(o_lo_ready, 1)
                if active(i, 0):
                    dve.wait_ge(xa_hi_ready, i + 1)
                    dve.wait_ge(val_psum, i)
                    dve.tensor_tensor(xa_lo[:], halves(B_TRET), xa_hi[:].bitcast(F32), ALU.subtract).then_inc(xa_lo_ready, 1)
                if active(i, 2):
                    gate(FFN2, f2)
                if active(i, -1):
                    mix(FFN1, i + 1)
                if active(i, 1):
                    dve.wait_ge(y_psum, a + 1)
                    if not isinstance(i, int) or a >= 2:
                        dve.wait_ge(xout_ready[FFN2], a - 1)
                    dve.tensor_tensor(x2[1 - k][:], halves(B_Y), x1[1 - k][:], ALU.add).then_inc(xout_ready[RET], 1)
                    dve.wait_ge(xout_ready[RET], a + 1)

            rounds(dve, one_round)

        @block.tensor
        def _(pe):
            def transpose_T(s, n):
                pe.wait_ge(xn_ready[s], 2 * n + 2)
                out = halves(B_T[s])
                for g in range(G):
                    for t in range(TILES):
                        mm = pe.transpose(out[:, g, t * P:(t + 1) * P], xn[s][:, t, g * P:(g + 1) * P], ident[:])
                mm.then_inc(xnT_psum[s], 1)

            def product_T(b, w, hi, lo):
                for m in range(G):
                    cols = slice(m * P, (m + 1) * P)
                    passes = [(w_hi[w], hi), (w_lo[w], hi), (w_hi[w], lo)]
                    for j, (g, (wt, xt)) in enumerate([(g, p) for g in range(G) for p in passes]):
                        mm = pe.matmul(halves(b)[:, m, :], wt[:, g, cols], xt[:, g, :], start=(j == 0), stop=(j == 5))
                return mm

            def product_rows(b, w, hi, lo):
                for t in range(TILES):
                    cols = slice(t * P, (t + 1) * P)
                    passes = [(hi, w_hi[w]), (hi, w_lo[w]), (lo, w_hi[w])]
                    for j, (g, (xt, wt)) in enumerate([(g, p) for g in range(G) for p in passes]):
                        mm = pe.matmul(halves(b)[:, t, :], xt[:, g, cols], wt[:, g, :], start=(j == 0), stop=(j == 5))
                return mm

            def hidden(f, n):
                pe.wait_ge(mix_hi[f], 2 * n + 1)
                pe.wait_ge(mix_lo[f], 2 * n + 1)
                product_T(B_HID[f], W_K, xk_hi[f], xk_lo[f]).then_inc(hid_psum[f], 1)

            def gate(f, n):
                pe.wait_ge(mix_hi[f], 2 * n + 2)
                pe.wait_ge(mix_lo[f], 2 * n + 2)
                product_rows(B_GATE[f], W_R, xr_hi[f], xr_lo[f]).then_inc(gate_psum[f], 1)

            def ffn_out(f, n):
                pe.wait_ge(ka_hi_ready[f], n + 1)
                pe.wait_ge(ka_lo_ready[f], n + 1)
                product_rows(B_OUT[f], W_V, ka_hi[f], ka_lo[f]).then_inc(out_psum[f], 1)

            def inter(c, n, first):
                pe.wait_ge(state_bd_ready, 2 * n + c)
                for g in range(G):
                    mm = pe.matmul(halves(B_OT)[:, g, c * P:(c + 1) * P], state_bd[:, g, :, :].rearrange("p h e -> p (h e)"),
                                   qdT[:, g, c * P:(c + 1) * P], start=(first and g == 0), stop=not first,
                                   skip_group_check=True)
                mm.then_inc(inter_done, 1)

            def outer(c, n):
                for g in range(G):
                    for r in range(HG):
                        cols = slice(g * P + r * HD, g * P + (r + 1) * HD)
                        mm = pe.matmul(bank[B_U[c]][r * HD:(r + 1) * HD, g * HD:(g + 1) * HD], krow[:, c, cols],
                                       vrow[:, c, cols], start=True, stop=True, skip_group_check=True)
                mm.then_inc(u_psum, 1)

            def weight_split(w):
                pe.wait_ge(w_hi_ready[w], 1)
                pe.wait_ge(w_lo_ready[w], 1)

            pe.wait_ge(ident_loaded, 16)
            transpose_T(FFN1, 0)

            def one_round(i, k):
                a, f2 = i - 1, i - 2
                if isinstance(i, int) and i == 0:
                    for w in (W_K, W_R, W_V):
                        weight_split(w)
                if isinstance(i, int) and i == 1:
                    for w in (W_Q, W_KEY, W_VAL, W_O):
                        weight_split(w)
                    pe.wait_ge(state_zeroed, 2)
                if active(i, 1):
                    pe.wait_ge(xa_lo_ready, a + 1)
                    product_T(B_Q, W_Q, xa_hi, xa_lo).then_inc(q_psum, 1)
                    if active(i, 0):
                        pe.wait_ge(xnT_ready[FFN1], i + 1)
                    product_T(B_KEY, W_KEY, xa_hi, xa_lo).then_inc(key_psum, 1)
                    pe.wait_ge(xout_ready[RET], a)
                    product_rows(B_VAL, W_VAL, xa_hi, xa_lo).then_inc(val_psum, 1)
                    pe.wait_ge(key_ready, a + 1)
                    if active(i, 2):
                        pe.wait_ge(gated[FFN2], f2)
                    for c in range(TILES):
                        for g in range(G):
                            mm = pe.transpose(halves(B_KROW)[:, c, g * P:(g + 1) * P], kT[:, g, c * P:(c + 1) * P], ident[:])
                    mm.then_inc(krow_psum, 1)
                if active(i, 0):
                    if active(i, 2):
                        pe.wait_ge(gate_ready[FFN2], f2)
                    hidden(FFN1, i)
                if active(i, 2):
                    pe.wait_ge(o_lo_ready, f2 + 1)
                    transpose_T(FFN2, f2)
                if active(i, 0):
                    gate(FFN1, i)
                if active(i, 1):
                    pe.wait_ge(val_ready, a + 1)
                    pe.wait_ge(krow_ready, a + 1)
                    for g in range(G):
                        for c in range(TILES):
                            for r in range(HG):
                                rows = slice(r * HD, (r + 1) * HD)
                                mm = pe.matmul(bank[B_SCORES + r][:, (g * TILES + c) * P:(g * TILES + c + 1) * P],
                                               kT[rows, g, c * P:(c + 1) * P], qT[rows, g, c * P:(c + 1) * P],
                                               start=True, stop=True)
                                if g == G - 1 and c == TILES - 1:
                                    mm.then_inc(scores_psum, 1)
                if active(i, 0):
                    if active(i, 1):
                        pe.wait_ge(state_ready, 2 * a)
                    ffn_out(FFN1, i)
                if active(i, 2):
                    if active(i, 0):
                        pe.wait_ge(gate_ready[FFN1], i + 1)
                    else:
                        pe.wait_ge(gate_ready[FFN2], f2)
                    hidden(FFN2, f2)
                    gate(FFN2, f2)
                if active(i, 1):
                    pe.wait_ge(qd_ready, a + 1)
                    if active(i, 2):
                        pe.wait_ge(xnT_ready[FFN2], f2 + 1)
                    inter(0, a, True)
                    pe.wait_ge(attn_ready, 4 * a + 1)
                    outer(0, a)
                if active(i, -1):
                    if active(i, 1):
                        pe.wait_ge(attn_ready, 4 * a + 2)
                    transpose_T(FFN1, i + 1)
                if active(i, 1):
                    pe.wait_ge(attn_ready, 4 * a + 4)
                    for c in range(TILES):
                        for g in range(G):
                            for r in range(HG):
                                mm = pe.matmul(halves(B_OT)[r * HD:(r + 1) * HD, g, c * P:(c + 1) * P],
                                               vrow[:, c, g * P + r * HD:g * P + (r + 1) * HD], attn[:, r, g, c, :],
                                               start=False, stop=(c == 0), skip_group_check=True)
                    if active(i, 0):
                        pe.wait_ge(gated[FFN1], i + 1)
                    inter(1, a, False)
                    outer(1, a)
                if active(i, 0):
                    if active(i, 1):
                        pe.wait_ge(state_ready, 2 * a + 1)
                    transpose_T(RET, i)
                if active(i, 2):
                    if not active(i, 1):
                        pe.wait_ge(gated[FFN2], f2)
                    ffn_out(FFN2, f2)
                if active(i, 1):
                    pe.wait_ge(o_lo_ready, a + 1)
                    product_rows(B_Y, W_O, o_hi, o_lo).then_inc(y_psum, 1)

            rounds(pe, one_round)


def tables():
    gamma = (1.0 - 2.0 ** (-5.0 - np.arange(HEADS))).astype(np.float64)
    head = np.arange(HEADS).reshape(G, HG)
    i = np.arange(P)
    diff = i[None, :] - i[:, None]
    lower = np.where(diff >= 0, gamma[:, None, None] ** np.maximum(diff, 0), 0.0)
    decay = np.stack([np.stack([lower[head[g, r]] for g in range(G)], 1) for r in range(HG)], 1)
    by_partition = np.repeat(head.T, HD, 0)
    decq = np.tile(gamma[by_partition][:, :, None] ** (i + 1), (1, 1, TILES))
    by_column = np.repeat(np.arange(HEADS), HD)
    deck = np.repeat((gamma[by_column][None, :] ** (P - 1 - i)[:, None])[:, None, :], TILES, 1)
    gstate = np.repeat((gamma[by_partition] ** P)[:, :, None], HD, 2)
    mask = (np.arange(P)[:, None, None] // HD == np.arange(HG)[None, :, None]) * np.ones((1, 1, HD))
    return [np.ascontiguousarray(t, dtype=np.float32) for t in (np.eye(P), decay, decq, deck, gstate, mask)]


def kernel(L0_attn_hidden_states, L0_attn_rel_pos, L0_attn_Wq, L0_attn_Wk, L0_attn_Wv, L0_attn_Wo,
           L0_ffn_W_r, L0_ffn_W_k, L0_ffn_W_v, L0_ffn_mu_r, L0_ffn_mu_k):
    import concourse.bacc as bacc
    from concourse.bass_utils import run_bass_kernel_spmd

    shape = L0_attn_hidden_states.shape
    x = np.ascontiguousarray(L0_attn_hidden_states).reshape(-1, D)
    weights = [np.ascontiguousarray(w) for w in (np.asarray(L0_ffn_W_r).T, np.asarray(L0_ffn_W_k).T, np.asarray(L0_ffn_W_v).T,
                                                 L0_attn_Wq, L0_attn_Wk, L0_attn_Wv, L0_attn_Wo)]
    mu = np.stack([np.asarray(L0_ffn_mu_r).reshape(G, P), np.asarray(L0_ffn_mu_k).reshape(G, P)])
    mu = np.ascontiguousarray(mu.transpose(2, 0, 1))
    arrays = {"x": x, "mu": mu}
    arrays.update({f"w{n}": w for n, w in enumerate(weights)})
    arrays.update(dict(zip(("ident", "decay", "decq", "deck", "gstate", "mask"), tables())))

    nc = bacc.Bacc("TRN2", target_bir_lowering=False, num_devices=1)
    aps = {n: nc.dram_tensor(f"in_{n}", a.shape, mybir.dt.from_np(a.dtype), kind="ExternalInput").ap() for n, a in arrays.items()}
    out = nc.dram_tensor("x_out", x.shape, F32, kind="ExternalOutput").ap()
    build(nc, aps["x"], [aps[f"w{n}"] for n in range(7)], aps["mu"], aps["ident"], aps["decay"], aps["decq"],
          aps["deck"], aps["gstate"], aps["mask"], out)
    r = run_bass_kernel_spmd(nc, [{f"in_{n}": a for n, a in arrays.items()}], core_ids=[0])
    return np.asarray(r.results[0]["x_out"]).reshape(shape)
```

```python
from contextlib import ExitStack

import numpy as np

import concourse.bass as bass
from concourse import mybir

F32 = mybir.dt.float32
F32R = mybir.dt.float32r
ALU = mybir.AluOpType
ACT = mybir.ActivationFunctionType

P = 128
D = 256
G = D // P
TILES = 2
BT = TILES * P
HEADS = 8
HD = D // HEADS
HG = P // HD
EPS = 1e-5
FFN1, RET, FFN2 = 0, 1, 2


def build(nc, x_in, weights, mu_in, ident_in, decay_in, decq_in, deck_in, gstate_in, mask_in, x_out):
    tokens = x_in.shape[0]
    NB = tokens // BT
    x_blocks = x_in.rearrange("(n t p) c -> n p t c", t=TILES, p=P)
    out_blocks = x_out.rearrange("(n t p) c -> n p t c", t=TILES, p=P)

    with ExitStack() as ctx:
        def sb(name, shape, dt=F32):
            return ctx.enter_context(nc.sbuf_tensor(name, [P] + shape, dt))

        def sem(name):
            return ctx.enter_context(nc.semaphore(name))

        def sem3(name):
            return [sem(f"{name}_{s}") for s in ("ffn1", "ret", "ffn2")]

        W_R, W_K, W_V, W_Q, W_KEY, W_VAL, W_O = range(7)
        w_f32 = [sb(f"w_f32_{w}", [G, D]) for w in range(7)]
        w_hi = [sb(f"w_hi_{w}", [G, D], F32R) for w in range(7)]
        w_lo = [sb(f"w_lo_{w}", [G, D], F32R) for w in range(7)]
        mu = sb("mu", [2, G])
        ident = sb("ident", [P])
        decay = sb("decay", [HG, G, P])
        decq = sb("decq", [G, BT])
        deck = sb("deck", [BT // P, D])
        gstate = sb("gstate", [G, HD])
        mask = sb("mask", [HG, HD])
        exponent = sb("exponent", [TILES])
        eps = sb("eps", [TILES])

        x0 = [sb(f"x0_{k}", [TILES, D]) for k in range(2)]
        x1 = [sb(f"x1_{k}", [TILES, D]) for k in range(2)]
        x2 = [sb(f"x2_{k}", [TILES, D]) for k in range(2)]
        y = sb("y", [TILES, D])

        stats = [sb(f"stats_{s}", [TILES, 6]) for s in range(3)]
        moments = [sb(f"moments_{s}", [TILES, 2]) for s in range(3)]
        var_eps = [sb(f"var_eps_{s}", [TILES]) for s in range(3)]
        rstd = [sb(f"rstd_{s}", [TILES]) for s in range(3)]
        xn = [sb(f"xn_{s}", [TILES, D]) for s in range(3)]

        def ffn(name, shape, dt=F32):
            return {f: sb(f"{name}_{f}", shape, dt) for f in (FFN1, FFN2)}

        xnT = ffn("xnT", [G, BT + 1])
        dT = ffn("dT", [G, BT])
        xkT, xrT = ffn("xkT", [G, BT]), ffn("xrT", [G, BT])
        xk_hi, xk_lo = ffn("xk_hi", [G, BT], F32R), ffn("xk_lo", [G, BT], F32R)
        xr_hi, xr_lo = ffn("xr_hi", [G, BT], F32R), ffn("xr_lo", [G, BT], F32R)
        reluT, sqT = ffn("reluT", [G, BT]), ffn("sqT", [G, BT])
        ka_hi, ka_lo = ffn("ka_hi", [G, BT], F32R), ffn("ka_lo", [G, BT], F32R)
        rgate, gatedx = ffn("rgate", [TILES, D]), ffn("gatedx", [TILES, D])

        xa_hi, xa_lo = sb("xa_hi", [G, BT], F32R), sb("xa_lo", [G, BT], F32R)
        qT, kT, qdT = sb("qT", [G, BT]), sb("kT", [G, BT]), sb("qdT", [G, BT])
        vrow, krow = sb("vrow", [TILES, D]), sb("krow", [TILES, D])
        attn = sb("attn", [HG, G, TILES, P])
        state = sb("state", [G, HD])
        state_bd = sb("state_bd", [G, HG, HD])
        state_dec = sb("state_dec", [G, HD])
        o_hi, o_lo = sb("o_hi", [G, BT], F32R), sb("o_lo", [G, BT], F32R)

        bank = [ctx.enter_context(nc.psum_tensor(f"bank{b}", [P, 512], F32)) for b in range(8)]

        def halves(b):
            return bank[b][:].rearrange("p (g t) -> p g t", g=2)

        B_Q, B_KEY, B_VAL, B_KROW = 0, 1, 2, 3
        B_HID1, B_GATE1, B_T2 = 4, 5, 6
        B_SCORES = 0
        B_OUT1, B_HID2, B_GATE2 = 7, 4, 5
        B_OT, B_T1, B_TRET, B_OUT2, B_Y = 6, 1, 0, 3, 2
        B_U = (0, 7)
        B_LAST_OUT = (3, 2)
        B_T = {FFN1: B_T1, RET: B_TRET, FFN2: B_T2}
        B_HID, B_GATE, B_OUT = {FFN1: B_HID1, FFN2: B_HID2}, {FFN1: B_GATE1, FFN2: B_GATE2}, {FFN1: B_OUT1, FFN2: B_OUT2}

        w_loaded = [sem(f"w_loaded{w}") for w in range(7)]
        ident_loaded, mu_loaded = sem("ident_loaded"), sem("mu_loaded")
        tables_loaded = sem("tables_loaded")
        w_hi_ready = [sem(f"w_hi_ready{w}") for w in range(7)]
        w_lo_ready = [sem(f"w_lo_ready{w}") for w in range(7)]
        halo_zeroed, state_zeroed = sem("halo_zeroed"), sem("state_zeroed")
        exponent_set, eps_set = sem("exponent_set"), sem("eps_set")
        x0_loaded, y_stored = sem("x0_loaded"), sem("y_stored")
        stats_ready = sem3("stats_ready")
        moments_ready = sem3("moments_ready")
        var_ready = sem3("var_ready")
        rstd_ready = sem3("rstd_ready")
        xn_ready = sem3("xn_ready")
        xnT_psum = sem3("xnT_psum")

        halo_ready, xnT_ready = sem3("halo_ready"), sem3("xnT_ready")
        d_ready = sem3("d_ready")
        mixed = sem3("mixed")
        xk_hi_ready, xr_hi_ready = sem3("xk_hi_ready"), sem3("xr_hi_ready")
        xk_lo_ready = sem3("xk_lo_ready")
        xr_lo_ready = sem3("xr_lo_ready")
        hid_psum, gate_psum, out_psum = sem3("hid_psum"), sem3("gate_psum"), sem3("out_psum")
        relu_ready, gate_ready = sem3("relu_ready"), sem3("gate_ready")
        sq_ready = sem3("sq_ready")
        ka_hi_ready, ka_lo_ready = sem3("ka_hi_ready"), sem3("ka_lo_ready")
        gated = sem3("gated")
        xout_ready = sem3("xout_ready")

        xnT_half, d_half = sem3("xnT_half"), sem3("d_half")
        xk_hi_half, xk_lo_half = sem3("xk_hi_half"), sem3("xk_lo_half")
        last_out_psum, last_gated, last_y = sem("last_out_psum"), sem("last_gated"), sem("last_y")

        xa_hi_ready, xa_lo_ready = sem("xa_hi_ready"), sem("xa_lo_ready")
        q_psum, key_psum, val_psum, krow_psum = sem("q_psum"), sem("key_psum"), sem("val_psum"), sem("krow_psum")
        q_ready, key_ready, val_ready = sem("q_ready"), sem("key_ready"), sem("val_ready")
        qd_ready = sem("qd_ready")
        krow_ready = sem("krow_ready")
        scores_psum = sem("scores_psum")
        attn_ready = sem("attn_ready")
        inter_done = sem("inter_done")
        u_psum = sem("u_psum")
        state_scaled = sem("state_scaled")
        state_ready = sem("state_ready")
        state_bd_ready = sem("state_bd_ready")
        y_psum = sem("y_psum")
        o_hi_ready, o_lo_ready = sem("o_hi_ready"), sem("o_lo_ready")

        def rounds(engine, one_round):
            for i in range(4):
                one_round(i, i % 2)
            with engine.Fori(2, NB // 2 - 1) as pair:
                one_round(2 * pair, 0)
                one_round(2 * pair + 1, 1)
            for i in range(NB - 2, NB + 2):
                one_round(i, i % 2)

        def active(i, lag):
            return not isinstance(i, int) or 0 <= i - lag < NB

        def first(i):
            return isinstance(i, int) and i == 0

        def second(i):
            return isinstance(i, int) and i == 1

        def last_retention(i):
            return isinstance(i, int) and i == NB

        def draining(i):
            return isinstance(i, int) and i == NB + 1

        def split(engine, w):
            engine.wait_ge(w_loaded[w], 16)
            engine.tensor_copy(w_hi[w][:], w_f32[w][:]).then_inc(w_hi_ready[w], 1)
            engine.wait_ge(w_hi_ready[w], 1)
            engine.tensor_tensor(w_lo[w][:], w_f32[w][:], w_hi[w][:].bitcast(F32), ALU.subtract).then_inc(w_lo_ready[w], 1)

        block = ctx.enter_context(nc.Block())

        @block.sync
        def _(sp):
            sp.dma_start(x0[0][:], x_blocks[0]).then_inc(x0_loaded, 16)
            for w in (W_K, W_R, W_V, W_Q, W_KEY, W_VAL, W_O):
                sp.dma_start(w_f32[w][:], weights[w].rearrange("(g p) d -> p g d", g=G)).then_inc(w_loaded[w], 16)
            sp.wait_ge(x0_loaded, 16)
            sp.dma_start(x0[1][:], x_blocks[1]).then_inc(x0_loaded, 16)
            for table, source in ((decq, decq_in), (deck, deck_in), (gstate, gstate_in), (mask, mask_in), (decay, decay_in)):
                sp.dma_start(table[:], source).then_inc(tables_loaded, 16)

            def one_round(i, k):
                if active(i, 0) and active(i, -2):
                    sp.wait_ge(xout_ready[FFN1], i + 1)
                    sp.wait_ge(x0_loaded, 16 * i + 32)
                    sp.dma_start(x0[k][:], x_blocks[i + 2]).then_inc(x0_loaded, 16)
                if active(i, 2):
                    n = i - 2
                    if draining(i):
                        for t in range(TILES):
                            sp.wait_ge(last_y, t + 1)
                            sp.dma_start(out_blocks[n][:, t, :], y[:, t, :]).then_inc(y_stored, 16)
                    else:
                        sp.wait_ge(xout_ready[FFN2], n + 1)
                        sp.dma_start(out_blocks[n], y[:]).then_inc(y_stored, 16)

            rounds(sp, one_round)
            sp.wait_ge(y_stored, 16 * (NB - 1) + 16 * TILES)

        @block.gpsimd
        def _(pool):
            pool.memset(exponent[:], -0.5).then_inc(exponent_set, 1)
            pool.memset(eps[:], EPS).then_inc(eps_set, 1)
            for s in (FFN1, FFN2):
                pool.memset(xnT[s][:, :, BT:BT + 1], 0.0).then_inc(halo_zeroed, 1)
            pool.memset(state[:], 0.0).then_inc(state_zeroed, 1)
            pool.memset(state_bd[:], 0.0).then_inc(state_zeroed, 1)
            pool.wait_ge(exponent_set, 1)
            pool.wait_ge(eps_set, 1)

            def inverse_std(s, n):
                pool.wait_ge(moments_ready[s], 2 * n + 2)
                pool.wait_ge(rstd_ready[s], n)
                pool.tensor_tensor(var_eps[s][:], moments[s][:, :, 1], eps[:], ALU.add).then_inc(var_ready[s], 1)
                pool.wait_ge(var_ready[s], n + 1)
                pool.wait_ge(xn_ready[s], 2 * n)
                pool.tensor_tensor(rstd[s][:], var_eps[s][:], exponent[:], ALU.pow).then_inc(rstd_ready[s], 1)

            def xk_low(f, n):
                pool.wait_ge(xk_hi_ready[f], n + 1)
                pool.wait_ge(hid_psum[f], n)
                pool.tensor_tensor(xk_lo[f][:], xkT[f][:], xk_hi[f][:].bitcast(F32), ALU.subtract).then_inc(xk_lo_ready[f], 1)

            def xr_low(f, n):
                pool.wait_ge(xr_hi_ready[f], n + 1)
                pool.wait_ge(gate_psum[f], n)
                pool.tensor_tensor(xr_lo[f][:], xrT[f][:], xr_hi[f][:].bitcast(F32), ALU.subtract).then_inc(xr_lo_ready[f], 1)

            def square_low(f, n):
                pool.wait_ge(sq_ready[f], n + 1)
                pool.wait_ge(ka_hi_ready[f], n + 1)
                pool.wait_ge(out_psum[f], n)
                pool.tensor_tensor(ka_lo[f][:], sqT[f][:], ka_hi[f][:].bitcast(F32), ALU.subtract).then_inc(ka_lo_ready[f], 1)

            def spread_state(c, n):
                pool.wait_ge(state_ready, 2 * n + c + 1)
                pool.wait_ge(inter_done, 2 * n + c + 1)
                pool.tensor_tensor(state_bd[:], state[:].unsqueeze(2).broadcast_to([P, G, HG, HD]),
                                   mask[:].unsqueeze(1).broadcast_to([P, G, HG, HD]), ALU.mult).then_inc(state_bd_ready, 1)

            inverse_std(FFN1, 0)
            split(pool, W_R)
            split(pool, W_V)
            inverse_std(FFN1, 1)
            xr_low(FFN1, 0)
            split(pool, W_KEY)
            pool.wait_ge(tables_loaded, 16 * 5)

            def one_round(i, k):
                a, f2 = i - 1, i - 2
                if active(i, 1):
                    pool.wait_ge(q_ready, a + 1)
                    pool.wait_ge(inter_done, 2 * a)
                    pool.tensor_tensor(qdT[:], qT[:], decq[:], ALU.mult).then_inc(qd_ready, 1)
                if active(i, -1) and not first(i):
                    inverse_std(FFN1, i + 1)
                if first(i):
                    xr_low(FFN1, 1)
                elif active(i, 0) and not second(i):
                    square_low(FFN1, i)
                if active(i, 2) and not draining(i):
                    xr_low(FFN2, f2)
                if active(i, 0):
                    inverse_std(RET, i)
                if active(i, 1):
                    spread_state(0, a)
                if active(i, 2) and not draining(i) and not last_retention(i):
                    square_low(FFN2, f2)
                if active(i, 1):
                    spread_state(1, a)
                if last_retention(i):
                    square_low(FFN2, f2)
                if last_retention(i):
                    inverse_std(FFN2, a)
                if active(i, 2) and not draining(i):
                    pool.wait_ge(gated[FFN2], f2 + 1)
                    pool.wait_ge(y_stored, 16 * f2)
                    pool.tensor_tensor(y[:], x2[k][:], gatedx[FFN2][:], ALU.add).then_inc(xout_ready[FFN2], 1)
                if active(i, -1) and not first(i):
                    xk_low(FFN1, i + 1)
                if active(i, 1) and not last_retention(i):
                    inverse_std(FFN2, a)
                if active(i, -1) and not first(i):
                    xr_low(FFN1, i + 1)

            rounds(pool, one_round)

        @block.scalar
        def _(act):
            act.dma_start(ident[:], ident_in).then_inc(ident_loaded, 16)
            act.dma_start(mu[:], mu_in).then_inc(mu_loaded, 16)
            act.preload_act_table(ACT.Sigmoid)

            def evacuate_T(f, n):
                act.wait_ge(xnT_psum[f], n + 1)
                act.wait_ge(mixed[f], 4 * n)
                act.wait_ge(xnT_ready[f], n)
                act.activation(xnT[f][:, :, 0:1], xnT[f][:, :, BT:BT + 1], ACT.Copy).then_inc(halo_ready[f], 1)
                act.wait_ge(halo_ready[f], n + 1)
                act.activation(xnT[f][:, :, 1:BT + 1], halves(B_T[f]), ACT.Copy).then_inc(xnT_ready[f], 1)

            def evacuate_T_by_halves(f, n):
                act.wait_ge(xnT_psum[f], n + 1)
                act.wait_ge(mixed[f], 4 * n)
                act.wait_ge(xnT_ready[f], n)
                act.activation(xnT[f][:, :, 0:1], xnT[f][:, :, BT:BT + 1], ACT.Copy).then_inc(halo_ready[f], 1)
                act.wait_ge(halo_ready[f], n + 1)
                act.activation(xnT[f][:, 0, 1:BT + 1], halves(B_T[f])[:, 0, :], ACT.Copy).then_inc(xnT_half[f], 1)
                act.activation(xnT[f][:, 1, 1:BT + 1], halves(B_T[f])[:, 1, :], ACT.Copy).then_inc(xnT_ready[f], 1)

            def mix_high_by_halves(f, n):
                act.wait_ge(hid_psum[f], n)
                for g, done in zip(range(G), (xk_hi_half[f], xk_hi_ready[f])):
                    act.wait_ge(mixed[f], 4 * n + g + 1)
                    act.activation(xk_hi[f][:, g, :], xkT[f][:, g, :], ACT.Copy).then_inc(done, 1)
                act.wait_ge(mixed[f], 4 * n + 4)
                act.wait_ge(gate_psum[f], n)
                act.activation(xr_hi[f][:], xrT[f][:], ACT.Copy).then_inc(xr_hi_ready[f], 1)

            def mix_high(f, n):
                act.wait_ge(mixed[f], 4 * n + 2)
                act.wait_ge(hid_psum[f], n)
                act.activation(xk_hi[f][:], xkT[f][:], ACT.Copy).then_inc(xk_hi_ready[f], 1)
                act.wait_ge(mixed[f], 4 * n + 4)
                act.wait_ge(gate_psum[f], n)
                act.activation(xr_hi[f][:], xrT[f][:], ACT.Copy).then_inc(xr_hi_ready[f], 1)

            def relu(f, n):
                act.wait_ge(hid_psum[f], n + 1)
                act.wait_ge(ka_hi_ready[f], n)
                act.activation(reluT[f][:], halves(B_HID[f]), ACT.Relu).then_inc(relu_ready[f], 1)

            def square(f, n):
                act.wait_ge(relu_ready[f], n + 1)
                act.wait_ge(ka_lo_ready[f], n)
                act.activation(sqT[f][:], reluT[f][:], ACT.Square).then_inc(sq_ready[f], 1)
                act.wait_ge(out_psum[f], n)
                act.activation(ka_hi[f][:], reluT[f][:], ACT.Square).then_inc(ka_hi_ready[f], 1)

            def sigmoid(f, n):
                act.wait_ge(gate_psum[f], n + 1)
                act.wait_ge(gated[f], n)
                act.activation(rgate[f][:], halves(B_GATE[f]), ACT.Sigmoid).then_inc(gate_ready[f], 1)

            act.wait_ge(halo_zeroed, 2)
            evacuate_T_by_halves(FFN1, 0)
            mix_high_by_halves(FFN1, 0)

            def one_round(i, k):
                a, f2 = i - 1, i - 2
                if active(i, 1):
                    act.wait_ge(q_psum, a + 1)
                    act.wait_ge(scores_psum, 4 * a)
                    act.wait_ge(qd_ready, a)
                    act.activation(qT[:], halves(B_Q), ACT.Copy, scale=HD ** -0.5).then_inc(q_ready, 1)
                    act.wait_ge(key_psum, a + 1)
                    act.activation(kT[:], halves(B_KEY), ACT.Copy).then_inc(key_ready, 1)
                    act.wait_ge(val_psum, a + 1)
                    act.wait_ge(u_psum, 2 * a)
                    act.activation(vrow[:], halves(B_VAL), ACT.Copy).then_inc(val_ready, 1)
                if active(i, 0) and not second(i):
                    relu(FFN1, i)
                if active(i, 2) and not draining(i):
                    evacuate_T(FFN2, f2)
                if first(i):
                    square(FFN1, 0)
                    evacuate_T(FFN1, 1)
                    sigmoid(FFN1, 0)
                elif active(i, 0) and not second(i):
                    square(FFN1, i)
                    sigmoid(FFN1, i)
                if draining(i):
                    evacuate_T_by_halves(FFN2, f2)
                    mix_high_by_halves(FFN2, f2)
                elif active(i, 2):
                    mix_high(FFN2, f2)
                if active(i, 2):
                    if not last_retention(i):
                        relu(FFN2, f2)
                        square(FFN2, f2)
                        sigmoid(FFN2, f2)
                if first(i):
                    mix_high(FFN1, 1)
                    relu(FFN1, 1)
                    square(FFN1, 1)
                    sigmoid(FFN1, 1)
                elif active(i, -1):
                    evacuate_T(FFN1, i + 1)
                if active(i, 1):
                    act.wait_ge(inter_done, 2 * a + 2)
                    act.wait_ge(y_psum, a)
                    act.activation(o_hi[:], halves(B_OT), ACT.Copy).then_inc(o_hi_ready, 1)
                if last_retention(i):
                    relu(FFN2, f2)
                    square(FFN2, f2)
                    sigmoid(FFN2, f2)
                if active(i, 0):
                    act.wait_ge(xnT_psum[RET], i + 1)
                    act.wait_ge(val_psum, i)
                    act.activation(xa_hi[:], halves(B_TRET), ACT.Copy).then_inc(xa_hi_ready, 1)
                if active(i, -1) and not first(i):
                    mix_high(FFN1, i + 1)

            rounds(act, one_round)

        @block.vector
        def _(dve):
            def layer_stats(s, n, x):
                stats_count = 2 * n + 2 if isinstance(n, int) else dve.to_reg(2 * n + 2)
                dve.wait_ge(moments_ready[s], 2 * n)
                dve.wait_ge(xn_ready[s], 2 * n)
                for t in range(TILES):
                    dve.bn_stats(stats[s][:, t, :], x[:, t, :]).then_inc(stats_ready[s], 1)
                dve.wait_ge(x0_loaded, 16)
                dve.wait_ge(stats_ready[s], stats_count)
                dve.wait_ge(xn_ready[s], 2 * n)
                for t in range(TILES):
                    dve.bn_aggr(moments[s][:, t, :], stats[s][:, t, :]).then_inc(moments_ready[s], 1)

            def normalize(s, n, x):
                dve.wait_ge(rstd_ready[s], n + 1)
                dve.wait_ge(xnT_psum[s], n)
                for t in range(TILES):
                    dve.tensor_scalar(xn[s][:, t, :], x[:, t, :], moments[s][:, t, 0:1], rstd[s][:, t:t + 1],
                                      ALU.subtract, ALU.mult).then_inc(xn_ready[s], 1)

            def mix(f, n):
                dve.wait_ge(xnT_ready[f], n + 1)
                dve.wait_ge(mixed[f], 4 * n)
                dve.tensor_tensor(dT[f][:], xnT[f][:, :, 1:BT + 1], xnT[f][:, :, 0:BT], ALU.subtract).then_inc(d_ready[f], 1)
                dve.wait_ge(d_ready[f], n + 1)
                dve.wait_ge(xk_lo_ready[f], n)
                dve.wait_ge(xr_lo_ready[f], n)
                for which, out in ((1, xkT[f]), (0, xrT[f])):
                    for g in range(G):
                        dve.scalar_tensor_tensor(out=out[:, g, :], in0=dT[f][:, g, :], scalar=mu[:, which, g:g + 1],
                                                 in1=xnT[f][:, g, 0:BT], op0=ALU.mult, op1=ALU.add).then_inc(mixed[f], 1)

            def xk_low(f, n):
                dve.wait_ge(xk_hi_ready[f], n + 1)
                dve.wait_ge(hid_psum[f], n)
                dve.tensor_tensor(xk_lo[f][:], xkT[f][:], xk_hi[f][:].bitcast(F32), ALU.subtract).then_inc(xk_lo_ready[f], 1)

            def xr_low(f, n):
                dve.wait_ge(xr_hi_ready[f], n + 1)
                dve.wait_ge(gate_psum[f], n)
                dve.tensor_tensor(xr_lo[f][:], xrT[f][:], xr_hi[f][:].bitcast(F32), ALU.subtract).then_inc(xr_lo_ready[f], 1)

            def mix_by_halves(f, n):
                def mixed_half(which, out, g):
                    dve.scalar_tensor_tensor(out=out[:, g, :], in0=dT[f][:, g, :], scalar=mu[:, which, g:g + 1],
                                             in1=xnT[f][:, g, 0:BT], op0=ALU.mult, op1=ALU.add).then_inc(mixed[f], 1)

                dve.wait_ge(mixed[f], 4 * n)
                dve.wait_ge(xk_lo_ready[f], n)
                dve.wait_ge(xr_lo_ready[f], n)
                for g, (into, done) in enumerate(((xnT_half[f], d_half[f]), (xnT_ready[f], d_ready[f]))):
                    count = 1 if g == 0 else n + 1
                    dve.wait_ge(into, count)
                    dve.tensor_tensor(dT[f][:, g, :], xnT[f][:, g, 1:BT + 1], xnT[f][:, g, 0:BT], ALU.subtract).then_inc(done, 1)
                    dve.wait_ge(done, count)
                    mixed_half(1, xkT[f], g)
                dve.wait_ge(hid_psum[f], n)
                for g, (into, done) in enumerate(((xk_hi_half[f], xk_lo_half[f]), (xk_hi_ready[f], xk_lo_ready[f]))):
                    dve.wait_ge(into, 1 if g == 0 else n + 1)
                    dve.tensor_tensor(xk_lo[f][:, g, :], xkT[f][:, g, :], xk_hi[f][:, g, :].bitcast(F32), ALU.subtract).then_inc(done, 1)
                for g in range(G):
                    mixed_half(0, xrT[f], g)

            def square_low(f, n):
                dve.wait_ge(sq_ready[f], n + 1)
                dve.wait_ge(ka_hi_ready[f], n + 1)
                dve.wait_ge(out_psum[f], n)
                dve.tensor_tensor(ka_lo[f][:], sqT[f][:], ka_hi[f][:].bitcast(F32), ALU.subtract).then_inc(ka_lo_ready[f], 1)

            def add_ffn1(n, k):
                dve.wait_ge(gated[FFN1], n + 1)
                if not isinstance(n, int) or n >= 2:
                    dve.wait_ge(xout_ready[RET], n - 1)
                dve.tensor_tensor(x1[k][:], x0[k][:], gatedx[FFN1][:], ALU.add).then_inc(xout_ready[FFN1], 1)

            def gate(f, n):
                dve.wait_ge(out_psum[f], n + 1)
                dve.wait_ge(gate_ready[f], n + 1)
                dve.wait_ge(xout_ready[f], n)
                dve.scalar_tensor_tensor(out=gatedx[f][:], in0=halves(B_OUT[f]), scalar=0.5, in1=rgate[f][:],
                                         op0=ALU.mult, op1=ALU.mult).then_inc(gated[f], 1)

            def mask_scores(n, begin, end):
                for r in range(begin, end):
                    dve.wait_ge(scores_psum, 4 * n + r + 1)
                    dve.wait_ge(inter_done, 2 * n)
                    dve.tensor_tensor(attn[:, r, :, :, :], bank[B_SCORES + r][:].rearrange("p (g c i) -> p g c i", g=G, c=TILES),
                                      decay[:, r, :, :].unsqueeze(2).broadcast_to([P, G, TILES, P]), ALU.mult).then_inc(attn_ready, 1)

            def scale_state(c, n):
                dve.wait_ge(state_ready, 2 * n + c)
                dve.tensor_tensor(state_dec[:], state[:], gstate[:], ALU.mult).then_inc(state_scaled, 1)

            def update_state(c, n):
                dve.wait_ge(state_bd_ready, 2 * n + c)
                dve.wait_ge(state_scaled, 2 * n + c + 1)
                dve.wait_ge(u_psum, 2 * n + c + 1)
                dve.tensor_tensor(state[:], bank[B_U[c]][:, 0:G * HD].rearrange("p (g e) -> p g e", g=G), state_dec[:],
                                  ALU.add).then_inc(state_ready, 1)

            dve.wait_ge(x0_loaded, 16)
            layer_stats(FFN1, 0, x0[0])
            normalize(FFN1, 0, x0[0])
            split(dve, W_K)
            dve.wait_ge(mu_loaded, 16)
            mix_by_halves(FFN1, 0)
            dve.wait_ge(x0_loaded, 32)
            layer_stats(FFN1, 1, x0[1])
            split(dve, W_Q)
            normalize(FFN1, 1, x0[1])
            square_low(FFN1, 0)
            mix(FFN1, 1)

            def one_round(i, k):
                a, f2 = i - 1, i - 2
                if second(i):
                    dve.wait_ge(tables_loaded, 16 * 5)
                if active(i, 1):
                    dve.wait_ge(krow_psum, a + 1)
                    dve.wait_ge(u_psum, 2 * a)
                    dve.tensor_tensor(krow[:], halves(B_KROW), deck[:], ALU.mult).then_inc(krow_ready, 1)
                if active(i, -1) and not first(i):
                    dve.wait_ge(x0_loaded, 16 * i + 32)
                    layer_stats(FFN1, i + 1, x0[1 - k])
                if draining(i):
                    mix_by_halves(FFN2, f2)
                    xr_low(FFN2, f2)
                elif active(i, 2):
                    mix(FFN2, f2)
                    xk_low(FFN2, f2)
                if active(i, -1) and not first(i):
                    normalize(FFN1, i + 1, x0[1 - k])
                if second(i):
                    dve.wait_ge(xout_ready[FFN1], 2)
                    layer_stats(RET, 1, x1[1])
                if active(i, 1):
                    mask_scores(a, 0, 2)
                if active(i, 0) and not second(i):
                    gate(FFN1, i)
                if active(i, 1):
                    mask_scores(a, 2, 3)
                if first(i):
                    xk_low(FFN1, 1)
                if active(i, 0) and not second(i):
                    add_ffn1(i, k)
                if active(i, 1):
                    scale_state(0, a)
                if active(i, 0) and not second(i):
                    dve.wait_ge(xout_ready[FFN1], i + 1)
                    layer_stats(RET, i, x1[k])
                if active(i, 1):
                    mask_scores(a, 3, 4)
                if active(i, 1):
                    update_state(0, a)
                if active(i, 0):
                    normalize(RET, i, x1[k])
                if first(i):
                    square_low(FFN1, 1)
                if active(i, 1):
                    scale_state(1, a)
                    update_state(1, a)
                    dve.wait_ge(o_hi_ready, a + 1)
                    dve.wait_ge(y_psum, a)
                    dve.tensor_tensor(o_lo[:], halves(B_OT), o_hi[:].bitcast(F32), ALU.subtract).then_inc(o_lo_ready, 1)
                if active(i, 0):
                    dve.wait_ge(xa_hi_ready, i + 1)
                    dve.wait_ge(val_psum, i)
                    dve.tensor_tensor(xa_lo[:], halves(B_TRET), xa_hi[:].bitcast(F32), ALU.subtract).then_inc(xa_lo_ready, 1)
                if first(i):
                    gate(FFN1, 1)
                    add_ffn1(1, 1)
                    split(dve, W_VAL)
                    split(dve, W_O)
                if draining(i):
                    square_low(FFN2, f2)
                if draining(i):
                    dve.wait_ge(gate_ready[FFN2], f2 + 1)
                    dve.wait_ge(xout_ready[FFN2], f2)
                    dve.wait_ge(y_stored, 16 * f2)
                    for t in range(TILES):
                        dve.wait_ge(last_out_psum, t + 1)
                        dve.scalar_tensor_tensor(out=gatedx[FFN2][:, t, :], in0=halves(B_LAST_OUT[t])[:, t, :], scalar=0.5,
                                                 in1=rgate[FFN2][:, t, :], op0=ALU.mult, op1=ALU.mult).then_inc(last_gated, 1)
                        dve.wait_ge(last_gated, t + 1)
                        dve.tensor_tensor(y[:, t, :], x2[k][:, t, :], gatedx[FFN2][:, t, :], ALU.add).then_inc(last_y, 1)
                elif active(i, 2) and not last_retention(i):
                    gate(FFN2, f2)
                if active(i, -1) and not first(i):
                    mix(FFN1, i + 1)
                if active(i, 1):
                    dve.wait_ge(y_psum, a + 1)
                    if not isinstance(i, int) or a >= 2:
                        dve.wait_ge(xout_ready[FFN2], a - 1)
                    dve.tensor_tensor(x2[1 - k][:], halves(B_Y), x1[1 - k][:], ALU.add).then_inc(xout_ready[RET], 1)
                    dve.wait_ge(xout_ready[RET], a + 1)
                    layer_stats(FFN2, a, x2[1 - k])
                    normalize(FFN2, a, x2[1 - k])
                    if last_retention(i):
                        gate(FFN2, f2)

            rounds(dve, one_round)

        @block.tensor
        def _(pe):
            def transpose_T(s, n):
                pe.wait_ge(xn_ready[s], 2 * n + 2)
                out = halves(B_T[s])
                for g in range(G):
                    for t in range(TILES):
                        mm = pe.transpose(out[:, g, t * P:(t + 1) * P], xn[s][:, t, g * P:(g + 1) * P], ident[:])
                mm.then_inc(xnT_psum[s], 1)

            def product_T(b, w, hi, lo):
                for m in range(G):
                    cols = slice(m * P, (m + 1) * P)
                    passes = [(w_hi[w], hi), (w_lo[w], hi), (w_hi[w], lo)]
                    for j, (g, (wt, xt)) in enumerate([(g, p) for g in range(G) for p in passes]):
                        mm = pe.matmul(halves(b)[:, m, :], wt[:, g, cols], xt[:, g, :], start=(j == 0), stop=(j == 5))
                return mm

            def product_rows(b, w, hi, lo, begin=0, end=TILES):
                for t in range(begin, end):
                    cols = slice(t * P, (t + 1) * P)
                    passes = [(hi, w_hi[w]), (hi, w_lo[w]), (lo, w_hi[w])]
                    for j, (g, (xt, wt)) in enumerate([(g, p) for g in range(G) for p in passes]):
                        mm = pe.matmul(halves(b)[:, t, :], xt[:, g, cols], wt[:, g, :], start=(j == 0), stop=(j == 5))
                return mm

            def hidden(f, n):
                pe.wait_ge(xk_hi_ready[f], n + 1)
                pe.wait_ge(xk_lo_ready[f], n + 1)
                product_T(B_HID[f], W_K, xk_hi[f], xk_lo[f]).then_inc(hid_psum[f], 1)

            def hidden_by_halves(f, n):
                for g in range(G):
                    pe.wait_ge(xk_hi_half[f], 1)
                    pe.wait_ge(xk_lo_half[f], 1)
                    if g == 1:
                        pe.wait_ge(xk_hi_ready[f], n + 1)
                        pe.wait_ge(xk_lo_ready[f], n + 1)
                    for m in range(G):
                        cols = slice(m * P, (m + 1) * P)
                        for j, (wt, xt) in enumerate([(w_hi[W_K], xk_hi[f]), (w_lo[W_K], xk_hi[f]), (w_hi[W_K], xk_lo[f])]):
                            mm = pe.matmul(halves(B_HID[f])[:, m, :], wt[:, g, cols], xt[:, g, :],
                                           start=(g == 0 and m == 0 and j == 0), stop=(g == 1 and j == 2), skip_group_check=True)
                mm.then_inc(hid_psum[f], 1)

            def gate(f, n, begin=0, end=TILES):
                if begin == 0:
                    pe.wait_ge(xr_hi_ready[f], n + 1)
                    pe.wait_ge(xr_lo_ready[f], n + 1)
                mm = product_rows(B_GATE[f], W_R, xr_hi[f], xr_lo[f], begin, end)
                if end == TILES:
                    mm.then_inc(gate_psum[f], 1)

            def ffn_out(f, n):
                pe.wait_ge(ka_hi_ready[f], n + 1)
                pe.wait_ge(ka_lo_ready[f], n + 1)
                product_rows(B_OUT[f], W_V, ka_hi[f], ka_lo[f]).then_inc(out_psum[f], 1)

            GROUPS = G * TILES

            def scores(n, begin, end):
                for group in range(begin, end):
                    g, c = group // TILES, group % TILES
                    for r in range(HG):
                        rows = slice(r * HD, (r + 1) * HD)
                        mm = pe.matmul(bank[B_SCORES + r][:, group * P:(group + 1) * P],
                                       kT[rows, g, c * P:(c + 1) * P], qT[rows, g, c * P:(c + 1) * P],
                                       start=True, stop=True)
                        if group == GROUPS - 1:
                            mm.then_inc(scores_psum, 1)

            def inter(c, n, first):
                pe.wait_ge(state_bd_ready, 2 * n + c)
                for g in range(G):
                    mm = pe.matmul(halves(B_OT)[:, g, c * P:(c + 1) * P], state_bd[:, g, :, :].rearrange("p h e -> p (h e)"),
                                   qdT[:, g, c * P:(c + 1) * P], start=(first and g == 0), stop=not first,
                                   skip_group_check=True)
                mm.then_inc(inter_done, 1)

            def outer(c, n):
                for g in range(G):
                    for r in range(HG):
                        cols = slice(g * P + r * HD, g * P + (r + 1) * HD)
                        mm = pe.matmul(bank[B_U[c]][r * HD:(r + 1) * HD, g * HD:(g + 1) * HD], krow[:, c, cols],
                                       vrow[:, c, cols], start=True, stop=True, skip_group_check=True)
                mm.then_inc(u_psum, 1)

            def keep_warm(b, count):
                for _ in range(count):
                    pe.matmul(bank[b][:, 0:D], w_hi[W_K][:, 0, 0:P], w_hi[W_K][:, 0, :], start=True, stop=True)

            def weight_split(w):
                pe.wait_ge(w_hi_ready[w], 1)
                pe.wait_ge(w_lo_ready[w], 1)

            pe.wait_ge(ident_loaded, 16)
            transpose_T(FFN1, 0)

            def one_round(i, k):
                a, f2 = i - 1, i - 2
                if first(i):
                    pe.wait_ge(w_hi_ready[W_K], 1)
                    keep_warm(B_Y, 24)
                    weight_split(W_K)
                if second(i):
                    pe.wait_ge(state_zeroed, 2)
                if active(i, 1):
                    pe.wait_ge(xa_lo_ready, a + 1)
                    if second(i):
                        weight_split(W_Q)
                    product_T(B_Q, W_Q, xa_hi, xa_lo).then_inc(q_psum, 1)
                    if active(i, 0):
                        pe.wait_ge(xnT_ready[FFN1], i + 1)
                    if second(i):
                        weight_split(W_KEY)
                    product_T(B_KEY, W_KEY, xa_hi, xa_lo).then_inc(key_psum, 1)
                    pe.wait_ge(xout_ready[RET], a)
                    if second(i):
                        weight_split(W_VAL)
                    product_rows(B_VAL, W_VAL, xa_hi, xa_lo).then_inc(val_psum, 1)
                    pe.wait_ge(key_ready, a + 1)
                    if active(i, 2):
                        pe.wait_ge(gated[FFN2], f2)
                    for c in range(TILES):
                        for g in range(G):
                            mm = pe.transpose(halves(B_KROW)[:, c, g * P:(g + 1) * P], kT[:, g, c * P:(c + 1) * P], ident[:])
                    mm.then_inc(krow_psum, 1)
                if active(i, 0) and not second(i):
                    if active(i, 2):
                        pe.wait_ge(gate_ready[FFN2], f2)
                    if first(i):
                        hidden_by_halves(FFN1, 0)
                    else:
                        hidden(FFN1, i)
                if first(i):
                    transpose_T(FFN1, 1)
                    weight_split(W_R)
                if active(i, 2):
                    pe.wait_ge(o_lo_ready, f2 + 1)
                    transpose_T(FFN2, f2)
                if active(i, 0) and not second(i):
                    gate(FFN1, i, 0, 1)
                if active(i, 1):
                    pe.wait_ge(val_ready, a + 1)
                    pe.wait_ge(krow_ready, a + 1)
                    scores(a, 0, 1)
                if active(i, 0) and not second(i):
                    gate(FFN1, i, 1, TILES)
                if first(i):
                    weight_split(W_V)
                if active(i, 1):
                    if second(i) or last_retention(i):
                        keep_warm(B_HID2, 8)
                    scores(a, 1, GROUPS)
                if active(i, 0) and not second(i):
                    if active(i, 1):
                        pe.wait_ge(state_ready, 2 * a)
                    ffn_out(FFN1, i)
                if first(i):
                    keep_warm(B_Y, 12)
                    pe.wait_ge(gate_ready[FFN1], 1)
                    hidden(FFN1, 1)
                    gate(FFN1, 1)
                if active(i, 2):
                    if active(i, 0):
                        pe.wait_ge(gate_ready[FFN1], i + 1)
                    else:
                        pe.wait_ge(gate_ready[FFN2], f2)
                    if draining(i):
                        keep_warm(B_KEY, 16)
                        hidden_by_halves(FFN2, f2)
                        gate(FFN2, f2)
                    elif not last_retention(i):
                        hidden(FFN2, f2)
                        gate(FFN2, f2)
                if active(i, 1):
                    pe.wait_ge(qd_ready, a + 1)
                    if active(i, 2):
                        pe.wait_ge(xnT_ready[FFN2], f2 + 1)
                    inter(0, a, True)
                    pe.wait_ge(attn_ready, 4 * a + 1)
                    outer(0, a)
                if active(i, -1) and not first(i):
                    if active(i, 1):
                        pe.wait_ge(attn_ready, 4 * a + 2)
                    transpose_T(FFN1, i + 1)
                if active(i, 1):
                    if last_retention(i):
                        keep_warm(B_HID2, 4)
                    for c in range(TILES):
                        for g in range(G):
                            for r in range(HG):
                                if c == 0 and g == 0:
                                    pe.wait_ge(attn_ready, 4 * a + r + 1)
                                mm = pe.matmul(halves(B_OT)[r * HD:(r + 1) * HD, g, c * P:(c + 1) * P],
                                               vrow[:, c, g * P + r * HD:g * P + (r + 1) * HD], attn[:, r, g, c, :],
                                               start=False, stop=(c == 0), skip_group_check=True)
                    if active(i, 0):
                        pe.wait_ge(gated[FFN1], i + 1)
                    inter(1, a, False)
                    outer(1, a)
                if active(i, 0):
                    if active(i, 1):
                        pe.wait_ge(state_ready, 2 * a + 1)
                    transpose_T(RET, i)
                if first(i):
                    pe.wait_ge(gated[FFN1], 1)
                    ffn_out(FFN1, 1)
                if last_retention(i):
                    hidden(FFN2, f2)
                elif active(i, 2):
                    if draining(i):
                        pe.wait_ge(gated[FFN2], f2)
                        pe.wait_ge(ka_hi_ready[FFN2], f2 + 1)
                        pe.wait_ge(ka_lo_ready[FFN2], f2 + 1)
                        for t in range(TILES):
                            product_rows(B_LAST_OUT[t], W_V, ka_hi[FFN2], ka_lo[FFN2], t, t + 1).then_inc(last_out_psum, 1)
                    else:
                        ffn_out(FFN2, f2)
                if active(i, 1):
                    pe.wait_ge(o_lo_ready, a + 1)
                    if second(i):
                        weight_split(W_O)
                    product_rows(B_Y, W_O, o_hi, o_lo).then_inc(y_psum, 1)
                if last_retention(i):
                    gate(FFN2, f2)
                    ffn_out(FFN2, f2)

            rounds(pe, one_round)


def tables():
    gamma = (1.0 - 2.0 ** (-5.0 - np.arange(HEADS))).astype(np.float64)
    head = np.arange(HEADS).reshape(G, HG)
    i = np.arange(P)
    diff = i[None, :] - i[:, None]
    lower = np.where(diff >= 0, gamma[:, None, None] ** np.maximum(diff, 0), 0.0)
    decay = np.stack([np.stack([lower[head[g, r]] for g in range(G)], 1) for r in range(HG)], 1)
    by_partition = np.repeat(head.T, HD, 0)
    decq = np.tile(gamma[by_partition][:, :, None] ** (i + 1), (1, 1, TILES))
    by_column = np.repeat(np.arange(HEADS), HD)
    deck = np.repeat((gamma[by_column][None, :] ** (P - 1 - i)[:, None])[:, None, :], TILES, 1)
    gstate = np.repeat((gamma[by_partition] ** P)[:, :, None], HD, 2)
    mask = (np.arange(P)[:, None, None] // HD == np.arange(HG)[None, :, None]) * np.ones((1, 1, HD))
    return [np.ascontiguousarray(t, dtype=np.float32) for t in (np.eye(P), decay, decq, deck, gstate, mask)]


def kernel(L0_attn_hidden_states, L0_attn_rel_pos, L0_attn_Wq, L0_attn_Wk, L0_attn_Wv, L0_attn_Wo,
           L0_ffn_W_r, L0_ffn_W_k, L0_ffn_W_v, L0_ffn_mu_r, L0_ffn_mu_k):
    import concourse.bacc as bacc
    from concourse.bass_utils import run_bass_kernel_spmd

    shape = L0_attn_hidden_states.shape
    x = np.ascontiguousarray(L0_attn_hidden_states).reshape(-1, D)
    weights = [np.ascontiguousarray(w) for w in (np.asarray(L0_ffn_W_r).T, np.asarray(L0_ffn_W_k).T, np.asarray(L0_ffn_W_v).T,
                                                 L0_attn_Wq, L0_attn_Wk, L0_attn_Wv, L0_attn_Wo)]
    mu = np.stack([np.asarray(L0_ffn_mu_r).reshape(G, P), np.asarray(L0_ffn_mu_k).reshape(G, P)])
    mu = np.ascontiguousarray(mu.transpose(2, 0, 1))
    arrays = {"x": x, "mu": mu}
    arrays.update({f"w{n}": w for n, w in enumerate(weights)})
    arrays.update(dict(zip(("ident", "decay", "decq", "deck", "gstate", "mask"), tables())))

    nc = bacc.Bacc("TRN2", target_bir_lowering=False, num_devices=1)
    aps = {n: nc.dram_tensor(f"in_{n}", a.shape, mybir.dt.from_np(a.dtype), kind="ExternalInput").ap() for n, a in arrays.items()}
    out = nc.dram_tensor("x_out", x.shape, F32, kind="ExternalOutput").ap()
    build(nc, aps["x"], [aps[f"w{n}"] for n in range(7)], aps["mu"], aps["ident"], aps["decay"], aps["decq"],
          aps["deck"], aps["gstate"], aps["mask"], out)
    r = run_bass_kernel_spmd(nc, [{f"in_{n}": a for n, a in arrays.items()}], core_ids=[0])
    return np.asarray(r.results[0]["x_out"]).reshape(shape)
```
